# Optimizing a Trainium2 kernel written in Bass

```python
import numpy as np
import jax
import jax.numpy as jnp

def _softmax(x, axis=-1):
    return jax.nn.softmax(x, axis=axis)

def _gelu(x):
    return jax.nn.gelu(x, approximate=True)

def _silu(x):
    return jax.nn.silu(x)

def _sigmoid(x):
    return jax.nn.sigmoid(x)

def _layernorm(x, axis=-1, eps=1e-05):
    m = jnp.mean(x, axis=axis, keepdims=True)
    v = jnp.var(x, axis=axis, keepdims=True)
    return (x - m) / jnp.sqrt(v + eps)

def _scatter_add(tgt, idx, src, axis=0):
    return tgt.at[idx].add(src)

def _segment_sum(src, seg, n):
    return jax.ops.segment_sum(src, seg, n)
kernel_name = 'mk_flamingo_gated_d1_seqx_r4_356e8e'

def setup_inputs(seed: int=0):
    np.random.seed(seed)
    _w = jnp.asarray

    def _rec_inputs():
        import jax
        import jax.numpy as jnp
        _rk = jax.random.key(seed)
        x = -0.000125 + 0.9999 * jax.random.normal(jax.random.fold_in(_rk, 1), (8, 256, 512), jnp.float32)
        _lenS = 256 - jax.random.randint(jax.random.fold_in(_rk, 7), (8,), 0, max(1, 256 // 4) + 1, jnp.int32)
        _lenS2 = 256 - jax.random.randint(jax.random.fold_in(_rk, 8), (8,), 0, max(1, 256 // 4) + 1, jnp.int32)
        _ctx_2048P = jax.random.normal(jax.random.fold_in(_rk, 11), (8, 16, 512), jnp.float32)
        _ctx_2048c = jax.random.dirichlet(jax.random.fold_in(_rk, 511), 0.3 * jnp.ones((16,), jnp.float32), (8, 256))
        _ctx_2048t = jnp.einsum('bsk,bkd->bsd', _ctx_2048c, _ctx_2048P)
        _ctx_2048t = _ctx_2048t * jax.lax.rsqrt(jnp.mean(jnp.square(_ctx_2048t)) + 1e-12) * 0.953939
        ctx_2048 = -1.52775e-05 + 0.999936 * (_ctx_2048t + 0.3 * jax.random.normal(jax.random.fold_in(_rk, 611), (8, 256, 512), jnp.float32))
        _g = jax.random.normal(jax.random.fold_in(_rk, 9001), (2, 1), jnp.float32)
        _g = jnp.sign(_g) * jnp.maximum(jnp.abs(_g), 1.0) + (_g == 0) * 1.0
        g_xattn = _g[0]
        g_ffn = _g[1]
        return (x, ctx_2048, g_xattn, g_ffn)
    x, ctx_2048, g_xattn, g_ffn = _rec_inputs()

    def _L0_xattn_setup():
        import jax, jax.numpy as jnp
        import numpy as np
        B, DIM1, DIM2, LATENT, T = (16, 256, 256, 128, 512)
        LN_EPS = 1e-05
        key = jax.random.key(seed)
        ks = jax.random.split(key, 8)

        def xavier(k, shape):
            fan_out, fan_in = shape
            std = float(np.sqrt(2.0 / (fan_in + fan_out)))
            return jax.random.normal(k, shape, dtype=jnp.float32) * std
        return {'input1': jax.random.normal(ks[0], (B, DIM1, T), dtype=jnp.float32), 'input2': jax.random.normal(ks[1], (B, DIM2, T), dtype=jnp.float32), 'theta_w': xavier(ks[2], (LATENT, DIM2)), 'theta_b': jnp.zeros((LATENT,), jnp.float32), 'phi_w': xavier(ks[3], (LATENT, DIM1)), 'phi_b': jnp.zeros((LATENT,), jnp.float32), 'g_w': xavier(ks[4], (LATENT, DIM1)), 'g_b': jnp.zeros((LATENT,), jnp.float32), 'ln_gamma': jnp.ones((LATENT, T), jnp.float32), 'ln_beta': jnp.zeros((LATENT, T), jnp.float32), 'out_w': xavier(ks[5], (DIM2, LATENT)), 'out_b': jnp.zeros((DIM2,), jnp.float32)}
    _L0_xattn_all = _L0_xattn_setup()
    _L0_xattn_in = {k: v for k, v in _L0_xattn_all.items() if k in ('theta_w', 'theta_b', 'phi_w', 'phi_b', 'g_w', 'g_b', 'ln_gamma', 'ln_beta', 'out_w', 'out_b')}
    del _L0_xattn_all

    def _L0_ffn_setup():
        import jax, jax.numpy as jnp
        import numpy as np
        GOLDEN_CENTER = 1.0 / np.e
        GOLDEN_LOWER = 0.5 - np.log(4.0 / 3.0)
        GOLDEN_UPPER = 0.5

        def _golden_weights(x, Wr, temperature):
            inh = jax.nn.sigmoid(x @ Wr / temperature)
            in_zone = (inh >= GOLDEN_LOWER) & (inh <= GOLDEN_UPPER)
            distance = jnp.abs(inh - GOLDEN_CENTER)
            weights = jnp.exp(-distance / 0.1) * in_zone.astype(x.dtype)
            wsum = jnp.sum(weights, axis=-1, keepdims=True)
            no_expert = wsum < 1e-08
            fb = jnp.exp(-distance / 0.3)
            _, top2 = jax.lax.top_k(fb, 2)
            fb_mask = jnp.sum(jax.nn.one_hot(top2, weights.shape[-1], dtype=x.dtype), axis=-2)
            fb_w = fb * fb_mask
            fb_w = fb_w / jnp.maximum(jnp.sum(fb_w, axis=-1, keepdims=True), 1e-08)
            weights = jnp.where(no_expert, fb_w, weights)
            weights = weights / jnp.maximum(jnp.sum(weights, axis=-1, keepdims=True), 1e-08)
            return weights
        key = jax.random.key(seed)
        ks = jax.random.split(key, 5)
        B, T, D, E, F = (2, 512, 512, 8, 512)
        s_in = 1.0 / np.sqrt(D)
        s_f = 1.0 / np.sqrt(F)
        return {'x': jax.random.normal(ks[0], (B, T, D), dtype=jnp.float32), 'Wg': jax.random.normal(ks[1], (E, D, F), dtype=jnp.float32) * s_in, 'Wu': jax.random.normal(ks[2], (E, D, F), dtype=jnp.float32) * s_in, 'Wd': jax.random.normal(ks[3], (E, F, D), dtype=jnp.float32) * s_f, 'Wr': jax.random.normal(ks[4], (D, E), dtype=jnp.float32) * s_in, 'temperature': jnp.ones((1,), dtype=jnp.float32)}
    _L0_ffn_all = _L0_ffn_setup()
    _L0_ffn_in = {k: v for k, v in _L0_ffn_all.items() if k in ('Wg', 'Wu', 'Wd', 'Wr', 'temperature')}
    del _L0_ffn_all
    return {'x': x, 'ctx_2048': ctx_2048, 'g_xattn': g_xattn, 'g_ffn': g_ffn, 'L0_xattn_theta_w': _L0_xattn_in['theta_w'], 'L0_xattn_theta_b': _L0_xattn_in['theta_b'], 'L0_xattn_phi_w': _L0_xattn_in['phi_w'], 'L0_xattn_phi_b': _L0_xattn_in['phi_b'], 'L0_xattn_g_w': _L0_xattn_in['g_w'], 'L0_xattn_g_b': _L0_xattn_in['g_b'], 'L0_xattn_ln_gamma': _L0_xattn_in['ln_gamma'], 'L0_xattn_ln_beta': _L0_xattn_in['ln_beta'], 'L0_xattn_out_w': _L0_xattn_in['out_w'], 'L0_xattn_out_b': _L0_xattn_in['out_b'], 'L0_ffn_Wg': _L0_ffn_in['Wg'], 'L0_ffn_Wu': _L0_ffn_in['Wu'], 'L0_ffn_Wd': _L0_ffn_in['Wd'], 'L0_ffn_Wr': _L0_ffn_in['Wr'], 'L0_ffn_temperature': _L0_ffn_in['temperature']}

def reference(x, ctx_2048, g_xattn, g_ffn, L0_xattn_theta_w, L0_xattn_theta_b, L0_xattn_phi_w, L0_xattn_phi_b, L0_xattn_g_w, L0_xattn_g_b, L0_xattn_ln_gamma, L0_xattn_ln_beta, L0_xattn_out_w, L0_xattn_out_b, L0_ffn_Wg, L0_ffn_Wu, L0_ffn_Wd, L0_ffn_Wr, L0_ffn_temperature):
    import jax
    import jax.numpy as jnp

    def _L0_xattn_ref(input1, input2, theta_w, theta_b, phi_w, phi_b, g_w, g_b, ln_gamma, ln_beta, out_w, out_b):
        import jax, jax.numpy as jnp
        import numpy as np
        B, DIM1, DIM2, LATENT, T = (16, 256, 256, 128, 512)
        LN_EPS = 1e-05
        theta_x = jnp.einsum('ld,bdt->btl', theta_w, input2) + theta_b
        phi_x = jnp.einsum('ld,bdt->blt', phi_w, input1) + phi_b[:, None]
        scores = jnp.einsum('btl,bls->bts', theta_x, phi_x)
        p = jax.nn.softmax(scores, axis=-1)
        g_x = jnp.einsum('ld,bdt->btl', g_w, input1) + g_b
        t_x = jnp.einsum('bts,bsl->blt', p, g_x)
        mu = jnp.mean(t_x, axis=(1, 2), keepdims=True)
        var = jnp.var(t_x, axis=(1, 2), keepdims=True)
        h = (t_x - mu) * jax.lax.rsqrt(var + LN_EPS) * ln_gamma + ln_beta
        h = jax.nn.relu(h)
        w_t = jnp.einsum('ol,blt->bot', out_w, h) + out_b[None, :, None]
        return w_t + input2

    def _L0_ffn_ref(x, Wg, Wu, Wd, Wr, temperature):
        import jax, jax.numpy as jnp
        import numpy as np
        GOLDEN_CENTER = 1.0 / np.e
        GOLDEN_LOWER = 0.5 - np.log(4.0 / 3.0)
        GOLDEN_UPPER = 0.5

        def _golden_weights(x, Wr, temperature):
            inh = jax.nn.sigmoid(x @ Wr / temperature)
            in_zone = (inh >= GOLDEN_LOWER) & (inh <= GOLDEN_UPPER)
            distance = jnp.abs(inh - GOLDEN_CENTER)
            weights = jnp.exp(-distance / 0.1) * in_zone.astype(x.dtype)
            wsum = jnp.sum(weights, axis=-1, keepdims=True)
            no_expert = wsum < 1e-08
            fb = jnp.exp(-distance / 0.3)
            _, top2 = jax.lax.top_k(fb, 2)
            fb_mask = jnp.sum(jax.nn.one_hot(top2, weights.shape[-1], dtype=x.dtype), axis=-2)
            fb_w = fb * fb_mask
            fb_w = fb_w / jnp.maximum(jnp.sum(fb_w, axis=-1, keepdims=True), 1e-08)
            weights = jnp.where(no_expert, fb_w, weights)
            weights = weights / jnp.maximum(jnp.sum(weights, axis=-1, keepdims=True), 1e-08)
            return weights
        weights = _golden_weights(x, Wr, temperature)
        gate = jnp.einsum('btd,edf->betf', x, Wg)
        up = jnp.einsum('btd,edf->betf', x, Wu)
        h = jax.nn.silu(gate) * up
        e_out = jnp.einsum('betf,efd->betd', h, Wd)
        out = jnp.einsum('bte,betd->btd', weights, e_out)
        return out
    x = x + jnp.tanh(g_xattn[0]) * _L0_xattn_ref(_layernorm(x, axis=-1), ctx_2048, L0_xattn_theta_w, L0_xattn_theta_b, L0_xattn_phi_w, L0_xattn_phi_b, L0_xattn_g_w, L0_xattn_g_b, L0_xattn_ln_gamma, L0_xattn_ln_beta, L0_xattn_out_w, L0_xattn_out_b)
    x = x + jnp.tanh(g_ffn[0]) * _L0_ffn_ref(_layernorm(x, axis=-1), L0_ffn_Wg, L0_ffn_Wu, L0_ffn_Wd, L0_ffn_Wr, L0_ffn_temperature)
    return x

_drawn_inputs = setup_inputs


def setup_inputs(seed=0):
    import zlib

    import numpy as np

    out = dict(_drawn_inputs(seed))
    spreads = {'L0_xattn_theta_b': (0.0, 0.1),
     'L0_xattn_phi_b': (0.0, 0.1),
     'L0_xattn_g_b': (0.0, 0.1),
     'L0_xattn_ln_gamma': (1.0, 0.2),
     'L0_xattn_ln_beta': (0.0, 0.1),
     'L0_xattn_out_b': (0.0, 0.1)}
    factors = {}
    for name, (base, spread) in spreads.items():
        noise = np.random.default_rng([zlib.crc32(name.encode()), seed]).standard_normal(out[name].shape)
        drawn = base * np.exp(spread * noise) if base else spread * noise
        out[name] = jnp.asarray(drawn.astype(out[name].dtype))
    for name, factor in factors.items():
        out[name] = (out[name] * factor).astype(out[name].dtype)
    return out
```

```python
import math
from contextlib import ExitStack

import concourse.bass as bass
from concourse import mybir

F32 = mybir.dt.float32
F16 = mybir.dt.float16
U32 = mybir.dt.uint32
ALU = mybir.AluOpType
ACT = mybir.ActivationFunctionType
AX = mybir.AxisListType
ABSMAX = bass.bass_isa.ReduceOp.absmax

P = 128
LN_EPS = 1e-5
GOLDEN_CENTER = 1.0 / math.e
GOLDEN_LOWER = 0.5 - math.log(4.0 / 3.0)
ZONE_LOW = math.log(GOLDEN_LOWER / (1.0 - GOLDEN_LOWER))
EXPONENT_BITS = 0x7F800000
XSCALE = 1024.0
TOP = 2.0 ** 14
TINY = 2.0 ** -100


def build(nc, x, ctx_in, g_xattn, g_ffn, theta_w, theta_b, phi_w, phi_b, g_w, g_b, ln_gamma, ln_beta,
          out_w, out_b, Wg, Wu, Wd, Wr, temperature, out):
    NB, C, T = x.shape
    L = theta_w.shape[0]
    E, D, F = Wg.shape
    CT = C // P
    TT = T // P
    KD = D // P
    KF = F // P
    NT = NB * CT
    TB = 512
    TPB = TB // P
    NBLK = NB * C // TB
    STEPS = E * NBLK
    PAIR = 2 * NBLK
    assert L == P and T == 512 and D == T and CT == 2 and NBLK == 4

    x_v = x.rearrange("b (j p) t -> b p j t", p=P)
    ctx_v = ctx_in.rearrange("b (j p) t -> b p j t", p=P)
    out_v = out.rearrange("b (j p) t -> p (b j) t", p=P)
    w_v = [w.rearrange("e (k p) n -> e p k n", p=P) for w in (Wg, Wu, Wd)]

    with ExitStack() as stack:
        def sb(name, shape, dt=F32):
            return stack.enter_context(nc.sbuf_tensor(name, shape, dt))

        def sem(name):
            return stack.enter_context(nc.semaphore(name))

        bank = [stack.enter_context(nc.psum_tensor(f"bank{i}", [P, 512], F32)) for i in range(8)]

        acc = sb("acc", [P, NT, T])
        xh = sb("xh", [P, KD, NB * C], F16)
        xl = sb("xl", [P, KD, NB * C], F16)
        ident = sb("ident", [P, P])
        mean_w = sb("mean_w", [P, P])
        neg_half = sb("neg_half", [P, 2])
        gate_raw = sb("gate_raw", [P, 3])
        gates = sb("gates", [P, 2])
        inv_temp = sb("inv_temp", [P, 1])
        logits = sb("logits", [P, NT, E])
        mix = sb("mix", [P, NT, E])

        wh1 = sb("wh1", [P, 3, KD, F], F16)
        wl1 = sb("wl1", [P, 3, KD, F], F16)

        def borrowed(of, w, tiles):
            return of[:, w:w + tiles // 2].rearrange("p w k n -> p (w k n)").bitcast(F32) \
                .rearrange("p (j t) -> p j t", t=T)

        prob = borrowed(wh1, 0, TT)
        in2 = borrowed(wh1, 2, CT)
        probT = borrowed(wl1, 0, TT)
        in1 = borrowed(wl1, 2, CT)
        res = sb("res", [P, CT, T])
        thetaT = sb("thetaT", [P, T])
        phi = sb("phi", [P, T])
        gx = sb("gx", [P, TT, L])
        tx = sb("tx", [P, T])
        z = sb("z", [P, T])
        hid = sb("hid", [P, T])
        xn2 = sb("xn2", [P, CT, T])
        gamma = sb("gamma", [P, T])
        beta = sb("beta", [P, T])
        proj_raw = sb("proj_raw", [P, 8, P])
        projT = sb("projT", [P, 8, P])
        theta_bc = sb("theta_bc", [P, 1])
        phi_bc = sb("phi_bc", [P, 1])
        g_bc = sb("g_bc", [P, 1])
        out_bc = sb("out_bc", [P, CT])
        st1 = sb("st1", [P, CT, 6])
        mv1 = sb("mv1", [P, CT, 2])
        ve1 = sb("ve1", [P, CT])
        rstd1 = sb("rstd1", [P, CT])
        st2 = sb("st2", [P, CT, 6])
        mv2 = sb("mv2", [P, CT, 2])
        ve2 = sb("ve2", [P, CT])
        rstd2 = sb("rstd2", [P, CT])
        nmr2 = sb("nmr2", [P, CT])
        sth = sb("sth", [P, 6])
        mvh = sb("mvh", [P, 2])
        muh = sb("muh", [P, 1])
        dh = sb("dh", [P, 1])
        vh = sb("vh", [P, 1])
        veh = sb("veh", [P, 1])
        rstdh = sb("rstdh", [P, 1])
        nmax = sb("nmax", [P, TT])
        rsum = sb("rsum", [P, TT])
        rinv = sb("rinv", [P, TT])
        wr_raw = sb("wr_raw", [P, KD, E])
        wr2 = sb("wr2", [P, KD, 2, E], F16)
        wrh, wrl = wr2[:, :, 0, :], wr2[:, :, 1, :]

        plane = sb("plane", [P, 10, NT, E])
        total = sb("total", [P, 6, NT])
        rank = sb("rank", [P, NT, E])

        wraw = sb("wraw", [P, 3, KD, F])
        wh = [sb("wh0", [P, 3, KD, F], F16), wh1]
        wl = [sb("wl0", [P, 3, KD, F], F16), wl1]
        silu = sb("silu", [P, 2, TB])
        hbuf = sb("hbuf", [P, KF, TB])
        hh = [sb(f"hh{i}", [P, KF, TB], F16) for i in range(2)]
        hl = [sb(f"hl{i}", [P, KF, TB], F16) for i in range(2)]
        ROUTER, WEIGHTS, HIDDEN = 0, 1, 3
        am = sb("am", [P, 5, 3])
        am_all = sb("am_all", [P, 5, 3])
        pow2 = sb("pow2", [P, 5, 3])
        scale = sb("scale", [P, 5, 3])
        unscale = sb("unscale", [P, 5, 3])
        ham = sb("ham", [P, KF])
        coef = sb("coef", [P, 2, TPB])

        ps_theta, ps_phi = bank[0], bank[1]
        ps_gx = bank[2]
        ps_out = [bank[3], bank[2]]
        ps_score = [bank[2], bank[3], bank[0], bank[1]]
        ps_tr = [bank[4], bank[5]]
        ps_tx = bank[6]
        ps_mu = bank[7][:, 0:1]
        ps_var = bank[7][:, 1:2]
        ps_router = bank[7][:, 16:16 + CT * 2 * E]
        ps_gate = [bank[0], bank[2]]
        ps_up = [bank[1], bank[3]]
        ps_down = [bank[4], bank[5], bank[6], bank[7]]

        const_ready = sem("const_ready")
        waits_met = sem("waits_met")
        ident_zero = sem("ident_zero")
        proj_loaded = sem("proj_loaded")
        bias_loaded = sem("bias_loaded")
        small_loaded = sem("small_loaded")
        gates_ready = sem("gates_ready")
        temp_ready = sem("temp_ready")
        projT_mm = sem("projT_mm")
        projT_ready = sem("projT_ready")
        wr_scaling = sem("wr_scaling")
        w_scaling = sem("w_scaling")
        h_scaling = sem("h_scaling")
        x_loaded = sem("x_loaded")
        in2_loaded = sem("in2_loaded")
        st1_done = sem("st1_done")
        mv1_done = sem("mv1_done")
        ve1_ready = sem("ve1_ready")
        rstd1_ready = sem("rstd1_ready")
        in1_ready = sem("in1_ready")
        res_ready = sem("res_ready")
        res_added = sem("res_added")
        theta_mm = sem("theta_mm")
        phi_mm = sem("phi_mm")
        theta_ready = sem("theta_ready")
        phi_ready = sem("phi_ready")
        score_mm = sem("score_mm")
        rowmax_ready = sem("rowmax_ready")
        exp_done = sem("exp_done")
        rinv_ready = sem("rinv_ready")
        prob_ready = sem("prob_ready")
        probT_mm = sem("probT_mm")
        probT_even = sem("probT_even")
        probT_odd = sem("probT_odd")
        gx_mm = sem("gx_mm")
        gx_ready = sem("gx_ready")
        tx_mm = sem("tx_mm")
        tx_ready = sem("tx_ready")
        sth_done = sem("sth_done")
        mvh_ready = sem("mvh_ready")
        mu_mm = sem("mu_mm")
        mu_read = sem("mu_read")
        vh_ready = sem("vh_ready")
        var_mm = sem("var_mm")
        veh_ready = sem("veh_ready")
        rstdh_ready = sem("rstdh_ready")
        z1_done = sem("z1_done")
        z2_done = sem("z2_done")
        hid_ready = sem("hid_ready")
        out_mm = sem("out_mm")
        acc_added = sem("acc_added")
        st2_done = sem("st2_done")
        mv2_done = sem("mv2_done")
        ve2_ready = sem("ve2_ready")
        rstd2_ready = sem("rstd2_ready")
        nmr2_ready = sem("nmr2_ready")
        xn2_ready = sem("xn2_ready")
        xT_mm = sem("xT_mm")
        xh_ready = sem("xh_ready")
        xl_ready = sem("xl_ready")
        router_mm = sem("router_mm")
        logits_ready = sem("logits_ready")
        wr_am = sem("wr_am")
        wr_am_all = sem("wr_am_all")
        wr_scaled = sem("wr_scaled")
        wrh_ready = sem("wrh_ready")
        wrl_ready = sem("wrl_ready")
        route_z = sem("route_z")
        route_exp = sem("route_exp")
        route_step = sem("route_step")
        route_dist = sem("route_dist")
        route_w = sem("route_w")
        mix_ready = sem("mix_ready")
        w_loaded = sem("w_loaded")
        w_am = sem("w_am")
        w_am_all = sem("w_am_all")
        w_scaled = sem("w_scaled")
        wh_ready = sem("wh_ready")
        wl_ready = sem("wl_ready")
        gate_mm = sem("gate_mm")
        up_mm = sem("up_mm")
        silu_ready = sem("silu_ready")
        h_done = sem("h_done")
        ham_done = sem("ham_done")
        h_am = sem("h_am")
        h_am_all = sem("h_am_all")
        h_scaled = sem("h_scaled")
        hh_ready = sem("hh_ready")
        hl_ready = sem("hl_ready")
        down_mm = sem("down_mm")
        coef_ready = sem("coef_ready")
        combined = sem("combined")
        stored = sem("stored")

        PROJ_LOADS, BIAS_LOADS, SMALL_LOADS = 4, 3, 8

        def at(i, turn):
            return isinstance(i, int) and i == turn

        def wait_apart(eng, signal, value):
            eng.wait_ge(signal, value)
            eng.sem_inc(waits_met, 1)

        block = stack.enter_context(nc.Block())

        LOOP_FROM, LOOP_TO, LAST_TURN = 4, NB - 1, NB + 2

        def turns(eng, turn, after=lambda i: None):
            for i in range(-1, LOOP_FROM):
                turn(i, lambda k, i=i: 0 <= i - k < NB)
            with eng.Fori(LOOP_FROM, LOOP_TO) as i:
                turn(i, lambda k: True)
            for i in range(LOOP_TO, LAST_TURN + 1):
                turn(i, lambda k, i=i: 0 <= i - k < NB)
                after(i)

        def steps(eng, first, turn):
            first()
            with eng.Fori(0, E // 2 - 1) as m:
                for u in range(PAIR):
                    turn(m * PAIR + u, m * 2 + u // NBLK, u, True)
            m = E // 2 - 1
            for u in range(PAIR):
                turn(m * PAIR + u, m * 2 + u // NBLK, u, u < PAIR - 1)

        @block.sync
        def _(sp):
            def load_x(b):
                if not isinstance(b, int) or b >= 1:
                    wait_apart(sp, x_loaded, b * 16)
                sp.dma_start(acc[:, bass.ds(b * CT, CT), :], x_v[b]).then_inc(x_loaded, 16)

            def load_in2(b):
                if not isinstance(b, int) or b >= 1:
                    wait_apart(sp, theta_mm, b)
                    wait_apart(sp, res_ready, b * CT)
                sp.dma_start(in2[:, :, :], ctx_v[b]).then_inc(in2_loaded, 16)

            load_x(0)
            load_in2(0)
            sp.dma_start(proj_raw[:, 0:2, :], theta_w.rearrange("l (k p) -> l k p", p=P)).then_inc(proj_loaded, 16)
            sp.dma_start(proj_raw[:, 2:4, :], phi_w.rearrange("l (k p) -> l k p", p=P)).then_inc(proj_loaded, 16)
            sp.dma_start(proj_raw[:, 4:6, :], g_w.rearrange("l (k p) -> l k p", p=P)).then_inc(proj_loaded, 16)
            sp.dma_start(proj_raw[:, 6:8, :], out_w.rearrange("(k p) l -> p k l", p=P)).then_inc(proj_loaded, 16)
            load_x(1)
            sp.wait_ge(theta_mm, 1)
            for i in range(3):
                sp.dma_start(wraw[:, i], w_v[i][0]).then_inc(w_loaded, 16)

            with sp.Fori(1, NB - 1) as b:
                load_in2(b)
                load_x(b + 1)
            load_in2(NB - 1)

            with sp.Fori(1, E) as e:
                sp.wait_ge(wh_ready, e * 3)
                wait_apart(sp, wl_ready, e * 3)
                for i in range(3):
                    sp.dma_start(wraw[:, i], w_v[i][e]).then_inc(w_loaded, 16)

            for blk in range(NBLK):
                for t in range(TPB):
                    sp.wait_ge(combined, (STEPS - NBLK + blk) * TPB + t + 1)
                    n = blk * TPB + t
                    sp.dma_start(out_v[:, n, :], acc[:, n, :]).then_inc(stored, 16)
            sp.wait_ge(stored, 16 * NT)

        @block.gpsimd
        def _(pool):
            nc.gpsimd.memset(ident[:], 0.0).then_inc(ident_zero, 1)
            nc.gpsimd.memset(mean_w[:], 1.0 / P).then_inc(const_ready, 1)
            nc.gpsimd.memset(neg_half[:], -0.5).then_inc(const_ready, 1)
            pool.wait_ge(ident_zero, 1)
            nc.gpsimd.affine_select(out=ident[:], in_=ident[:], compare_op=ALU.not_equal, fill=1.0, base=0,
                                    pattern=[[-1, P]], channel_multiplier=1).then_inc(const_ready, 1)
            for e in range(E):
                nc.gpsimd.memset(rank[:, :, e], float(E - e)).then_inc(const_ready, 1)
            pool.wait_ge(const_ready, 3)

            def turn(i, has):
                if has(2):
                    pool.wait_ge(veh_ready, i - 2 + 1)
                    nc.gpsimd.tensor_tensor(rstdh[:], veh[:], neg_half[:, 0:1], ALU.pow).then_inc(rstdh_ready, 1)
                if has(0):
                    if at(i, 0):
                        pool.wait_ge(gates_ready, 1)
                        pool.wait_ge(small_loaded, 16 * SMALL_LOADS)
                    if has(1):
                        wait_apart(pool, res_added, i * CT)
                    wait_apart(pool, in2_loaded, i * 16 + 16)
                    for j in range(CT):
                        nc.gpsimd.tensor_scalar(res[:, j], in2[:, j], out_bc[:, j:j + 1], gates[:, 0:1],
                                                ALU.add, ALU.mult).then_inc(res_ready, 1)
                    pool.wait_ge(in1_ready, i * CT + CT)
                    for j in range(CT):
                        pool.wait_ge(res_ready, i * CT + j + 1)
                        a = acc[:, bass.ds(i * CT + j, 1), :].rearrange("p a t -> p (a t)")
                        nc.gpsimd.tensor_tensor(a, a, res[:, j], ALU.add).then_inc(res_added, 1)
                if has(-1):
                    pool.wait_ge(ve1_ready, i + 2)
                    nc.gpsimd.tensor_tensor(rstd1[:], ve1[:], neg_half[:], ALU.pow).then_inc(rstd1_ready, 1)
                if has(2):
                    pool.wait_ge(ve2_ready, i - 2 + 1)
                    nc.gpsimd.tensor_tensor(rstd2[:], ve2[:], neg_half[:], ALU.pow).then_inc(rstd2_ready, 1)
                if at(i, 0):
                    pool.wait_ge(wr_am, 1)
                    nc.gpsimd.partition_all_reduce(am_all[:, ROUTER, 0:1], am[:, ROUTER, 0:1], P, ABSMAX) \
                        .then_inc(wr_am_all, 1)
                if at(i, 1):
                    all_reduce_weights(0, 0)

            def all_reduce_weights(e, par):
                wait_apart(pool, w_am, e * 3 + 3)
                nc.gpsimd.partition_all_reduce(am_all[:, WEIGHTS + par, :], am[:, WEIGHTS + par, :], P, ABSMAX) \
                    .then_inc(w_am_all, 1)

            def all_reduce_hidden(s, hp):
                wait_apart(pool, h_am, s + 1)
                nc.gpsimd.partition_all_reduce(am_all[:, HIDDEN + hp, 0:1], am[:, HIDDEN, 0:1], P, ABSMAX) \
                    .then_inc(h_am_all, 1)

            def step_turn(s, e, u, more):
                if more:
                    all_reduce_hidden(s + 1, (u + 1) % 2)
                if u % NBLK == 0 and not at(e, E - 1):
                    all_reduce_weights(e + 1, (u // NBLK + 1) % 2)

            turns(pool, turn)
            steps(pool, lambda: all_reduce_hidden(0, 0), step_turn)

        def proj_w(which, k):
            return projT[:, 2 * which + k, :]

        @block.scalar
        def _(act):
            act.dma_start(theta_bc[:], theta_b.rearrange("(l a) -> l a", a=1)).then_inc(bias_loaded, 16)
            act.dma_start(phi_bc[:], phi_b.rearrange("(l a) -> l a", a=1)).then_inc(bias_loaded, 16)
            act.dma_start(g_bc[:], g_b.rearrange("(l a) -> l a", a=1)).then_inc(bias_loaded, 16)
            for dst, src in ((gate_raw[:, 0:1], g_xattn), (gate_raw[:, 1:2], g_ffn), (gate_raw[:, 2:3], temperature)):
                act.dma_start(dst, src.partition_broadcast(P)).then_inc(small_loaded, 16)
            for j in range(CT):
                act.dma_start(out_bc[:, j:j + 1], out_b[j * P:(j + 1) * P].rearrange("(l a) -> l a", a=1)) \
                    .then_inc(small_loaded, 16)
            act.dma_start(gamma[:], ln_gamma).then_inc(small_loaded, 16)
            act.dma_start(beta[:], ln_beta).then_inc(small_loaded, 16)
            act.dma_start(wr_raw[:], Wr.rearrange("(k p) e -> p k e", p=P)).then_inc(small_loaded, 16)
            for n in range(2):
                act.wait_ge(projT_mm, n + 1)
                nc.scalar.copy(projT[:, 4 * n:4 * n + 4, :].rearrange("p a l -> p (a l)"), ps_tr[n][:]) \
                    .then_inc(projT_ready, 1)

            def turn(i, has):
                if has(0):
                    act.wait_ge(theta_mm, i + 1)
                    if has(1):
                        act.wait_ge(score_mm, i * TT)
                    nc.scalar.activation(thetaT[:], ps_theta[:], ACT.Identity, bias=theta_bc[:]) \
                        .then_inc(theta_ready, 1)
                    act.wait_ge(phi_mm, i + 1)
                    nc.scalar.activation(phi[:], ps_phi[:], ACT.Identity, bias=phi_bc[:]).then_inc(phi_ready, 1)
                if at(i, 0):
                    act.wait_ge(small_loaded, 16 * SMALL_LOADS)
                    nc.scalar.activation(gates[:], gate_raw[:, 0:2], ACT.Tanh).then_inc(gates_ready, 1)
                if has(1):
                    for j in range(0, TT, 2):
                        act.wait_ge(probT_mm, (i - 1) * TT + j + 1)
                        if has(2):
                            act.wait_ge(tx_mm, i - 1)
                        nc.scalar.copy(probT[:, j], ps_tr[j % 2][:]).then_inc(probT_even, 1)
                if has(3):
                    act.wait_ge(nmr2_ready, i - 2)
                    for j in range(CT):
                        a = acc[:, bass.ds((i - 3) * CT + j, 1), :].rearrange("p a t -> p (a t)")
                        nc.scalar.activation(xn2[:, j], a, ACT.Identity, bias=nmr2[:, j:j + 1],
                                             scale=rstd2[:, j:j + 1]).then_inc(xn2_ready, 1)
                if has(0):
                    if has(1):
                        act.wait_ge(probT_mm, i * TT)
                        act.wait_ge(rinv_ready, i)
                    for j in range(TT):
                        act.wait_ge(rowmax_ready, i * TT + j + 1)
                        nc.scalar.activation(prob[:, j], ps_score[j][:], ACT.Exp, bias=nmax[:, j:j + 1],
                                             accum_out=rsum[:, j:j + 1]).then_inc(exp_done, 1)
                if has(2):
                    act.wait_ge(z2_done, i - 1)
                    if has(3):
                        act.wait_ge(out_mm, (i - 2) * CT)
                    nc.scalar.activation(hid[:], z[:], ACT.Relu).then_inc(hid_ready, 1)
                if has(1):
                    act.wait_ge(tx_mm, i)
                    if has(2):
                        act.wait_ge(z1_done, i - 1)
                    nc.scalar.activation(tx[:], ps_tx[:], ACT.Identity, bias=g_bc[:]).then_inc(tx_ready, 1)
                if has(0):
                    act.wait_ge(gx_mm, i + 1)
                    if has(1):
                        act.wait_ge(tx_mm, i)
                    nc.scalar.copy(gx[:].rearrange("p a l -> p (a l)"), ps_gx[:]).then_inc(gx_ready, 1)
                if has(3):
                    for m in range(2):
                        act.wait_ge(xT_mm, (i - 3) * 2 + m + 1)
                        nc.scalar.activation(
                            xh[:, 2 * m:2 * m + 2, bass.ds((i - 3) * C, C)],
                            ps_tr[m][:].rearrange("p (k c) -> p k c", k=2), ACT.Copy, scale=XSCALE) \
                            .then_inc(xh_ready, 1)
                if at(i, 0):
                    act.wait_ge(wr_scaled, 1)
                    nc.scalar.activation(wrh, wr_raw[:], ACT.Copy, scale=scale[:, ROUTER, 0:1]) \
                        .then_inc(wrh_ready, 1)
                if at(i, 2):
                    for w in range(3):
                        weights_high(0, 0, w)

            def weights_high(e, par, w):
                act.wait_ge(w_scaled, e + 1)
                nc.scalar.activation(wh[par][:, w], wraw[:, w], ACT.Copy, scale=scale[:, WEIGHTS + par, w:w + 1]) \
                    .then_inc(wh_ready, 1)

            act.wait_ge(bias_loaded, 16 * BIAS_LOADS)
            turns(act, turn)

            act.wait_ge(route_z, 1)
            nc.scalar.activation(plane[:, 1], plane[:, 0], ACT.Exp, scale=-1.0).then_inc(route_exp, 1)
            act.wait_ge(route_dist, 1)
            nc.scalar.activation(plane[:, 4], plane[:, 3], ACT.Exp, scale=-1.0 / 0.1).then_inc(route_exp, 1)
            nc.scalar.activation(plane[:, 5], plane[:, 3], ACT.Exp, scale=-1.0 / 0.3).then_inc(route_exp, 1)

            def silu_of(s, par):
                for f in range(KF):
                    act.wait_ge(gate_mm, s * KF + f + 1)
                    if not isinstance(s, int) or s * KF + f >= 2:
                        act.wait_ge(h_done, s * KF + f - 1)
                    nc.scalar.activation(silu[:, f % 2], ps_gate[f % 2][:], ACT.Silu, scale=unscale[:, WEIGHTS + par, 0:1]) \
                        .then_inc(silu_ready, 1)

            def hidden_high(s, hp):
                act.wait_ge(h_scaled, s + 1)
                nc.scalar.activation(hh[hp][:], hbuf[:], ACT.Copy, scale=scale[:, HIDDEN + hp, 0:1]) \
                    .then_inc(hh_ready, 1)

            def step_turn(s, e, u, more):
                last = at(e, E - 1)
                if more:
                    silu_of(s + 1, (u + 1) // NBLK % 2)
                    hidden_high(s + 1, (u + 1) % 2)
                if u % NBLK == 1 and not last:
                    act.wait_ge(gate_mm, s * KF + KF)
                    for w in range(3):
                        weights_high(e + 1, (u // NBLK + 1) % 2, w)

            steps(act, lambda: (silu_of(0, 0), hidden_high(0, 0)), step_turn)

        @block.vector
        def _(dve):
            def power_scale(slot, n, scaling, turn, extra):
                sl, seen = slice(0, n), turn * 4
                nc.vector.tensor_scalar(am_all[:, slot, sl], am_all[:, slot, sl], TINY, None, ALU.max) \
                    .then_inc(scaling, 1)
                dve.wait_ge(scaling, seen + 1)
                nc.vector.tensor_scalar(pow2[:, slot, sl].bitcast(U32), am_all[:, slot, sl].bitcast(U32),
                                        EXPONENT_BITS, None, ALU.bitwise_and).then_inc(scaling, 1)
                dve.wait_ge(scaling, seen + 2)
                nc.vector.reciprocal(scale[:, slot, sl], pow2[:, slot, sl]).then_inc(scaling, 1)
                nc.vector.tensor_scalar(unscale[:, slot, sl], pow2[:, slot, sl], extra / TOP, None, ALU.mult) \
                    .then_inc(scaling, 1)
                dve.wait_ge(scaling, seen + 4)
                return nc.vector.tensor_scalar(scale[:, slot, sl], scale[:, slot, sl], TOP, None, ALU.mult)

            def router_weights():
                nc.vector.reciprocal(inv_temp[:], gate_raw[:, 2:3]).then_inc(temp_ready, 1)
                nc.vector.tensor_reduce(am[:, 0, 0:1], wr_raw[:].rearrange("p k e -> p (k e)"), AX.X, ALU.max,
                                        apply_absolute_value=True).then_inc(wr_am, 1)
                dve.wait_ge(wr_am_all, 1)
                power_scale(ROUTER, 1, wr_scaling, 0, 1.0 / XSCALE).then_inc(wr_scaled, 1)
                dve.wait_ge(wr_scaled, 1)
                dve.wait_ge(wrh_ready, 1)
                nc.vector.scalar_tensor_tensor(wrl, wr_raw[:], scale[:, ROUTER, 0:1], wrh, ALU.mult,
                                               ALU.subtract).then_inc(wrl_ready, 1)

            def weights_max(e, par):
                dve.wait_ge(w_loaded, e * 48 + 48)
                for w in range(3):
                    nc.vector.tensor_reduce(am[:, WEIGHTS + par, w:w + 1], wraw[:, w].rearrange("p k n -> p (k n)"),
                                            AX.X, ALU.max, apply_absolute_value=True).then_inc(w_am, 1)

            def weights_scale(e, par):
                dve.wait_ge(w_am_all, e + 1)
                power_scale(WEIGHTS + par, 3, w_scaling, e, 1.0 / XSCALE).then_inc(w_scaled, 1)

            def weights_low(e, par, which=(0, 1, 2)):
                dve.wait_ge(w_scaled, e + 1)
                for w in which:
                    dve.wait_ge(wh_ready, e * 3 + w + 1)
                    nc.vector.scalar_tensor_tensor(
                        wl[par][:, w].rearrange("p k n -> p (k n)"), wraw[:, w].rearrange("p k n -> p (k n)"),
                        scale[:, WEIGHTS + par, w:w + 1], wh[par][:, w].rearrange("p k n -> p (k n)"),
                        ALU.mult, ALU.subtract).then_inc(wl_ready, 1)

            def turn(i, has):
                if has(2):
                    dve.wait_ge(var_mm, i - 1)
                    nc.vector.tensor_scalar(veh[:], ps_var, LN_EPS, None, ALU.add).then_inc(veh_ready, 1)
                    if has(3):
                        dve.wait_ge(hid_ready, i - 2)
                    nc.vector.scalar_tensor_tensor(z[:], tx[:], muh[:], gamma[:], ALU.subtract, ALU.mult) \
                        .then_inc(z1_done, 1)
                if has(1):
                    for j in range(1, TT, 2):
                        dve.wait_ge(probT_mm, (i - 1) * TT + j + 1)
                        if has(2):
                            dve.wait_ge(tx_mm, i - 1)
                        nc.vector.tensor_copy(probT[:, j], ps_tr[j % 2][:]).then_inc(probT_odd, 1)
                if has(2):
                    dve.wait_ge(rstdh_ready, i - 1)
                    dve.wait_ge(z1_done, i - 1)
                    nc.vector.scalar_tensor_tensor(z[:], z[:], rstdh[:], beta[:], ALU.mult, ALU.add) \
                        .then_inc(z2_done, 1)
                if has(0):
                    for j in range(TT):
                        dve.wait_ge(score_mm, i * TT + j + 1)
                        nc.vector.tensor_reduce(nmax[:, j:j + 1], ps_score[j][:], AX.X, ALU.max,
                                                negate=True).then_inc(rowmax_ready, 1)
                if has(-1):
                    wait_apart(dve, x_loaded, i * 16 + 32)
                    for j in range(CT):
                        a = acc[:, bass.ds((i + 1) * CT + j, 1), :].rearrange("p a t -> p (a t)")
                        nc.vector.bn_stats(st1[:, j], a).then_inc(st1_done, 1)
                    for j in range(CT):
                        wait_apart(dve, st1_done, (i + 1) * CT + j + 1)
                        nc.vector.bn_aggr(mv1[:, j], st1[:, j]).then_inc(mv1_done, 1)
                    dve.wait_ge(mv1_done, (i + 2) * CT)
                    nc.vector.tensor_scalar(ve1[:], mv1[:, :, 1], LN_EPS, None, ALU.add).then_inc(ve1_ready, 1)
                if has(0):
                    dve.wait_ge(exp_done, i * TT + TT)
                    nc.vector.reciprocal(rinv[:], rsum[:]).then_inc(rinv_ready, 1)
                    dve.wait_ge(rinv_ready, i + 1)
                    for j in range(TT):
                        nc.vector.tensor_scalar(prob[:, j], prob[:, j], rinv[:, j:j + 1], None, ALU.mult) \
                            .then_inc(prob_ready, 1)
                if has(1):
                    wait_apart(dve, tx_ready, i)
                    nc.vector.bn_stats(sth[:], tx[:]).then_inc(sth_done, 1)
                    wait_apart(dve, sth_done, i)
                    nc.vector.bn_aggr(mvh[:], sth[:]).then_inc(mvh_ready, 1)
                if has(-1):
                    dve.wait_ge(rstd1_ready, i + 2)
                    if has(0):
                        dve.wait_ge(gx_mm, i + 1)
                    for j in range(CT):
                        a = acc[:, bass.ds((i + 1) * CT + j, 1), :].rearrange("p a t -> p (a t)")
                        nc.vector.tensor_scalar(in1[:, j], a, mv1[:, j, 0:1], rstd1[:, j:j + 1], ALU.subtract,
                                                ALU.mult).then_inc(in1_ready, 1)
                if has(1):
                    dve.wait_ge(mu_mm, i)
                    nc.vector.tensor_copy(muh[:], ps_mu).then_inc(mu_read, 1)
                    dve.wait_ge(mu_read, i * 2 - 1)
                    nc.vector.tensor_tensor(dh[:], mvh[:, 0:1], muh[:], ALU.subtract).then_inc(mu_read, 1)
                    dve.wait_ge(mu_read, i * 2)
                    nc.vector.scalar_tensor_tensor(vh[:], dh[:], dh[:], mvh[:, 1:2], ALU.mult, ALU.add) \
                        .then_inc(vh_ready, 1)
                if has(3):
                    for m in range(2):
                        dve.wait_ge(xh_ready, (i - 3) * 2 + m + 1)
                        where = (slice(None), slice(2 * m, 2 * m + 2), bass.ds((i - 3) * C, C))
                        nc.vector.scalar_tensor_tensor(
                            xl[where], ps_tr[m][:].rearrange("p (k c) -> p k c", k=2), XSCALE, xh[where],
                            ALU.mult, ALU.subtract).then_inc(xl_ready, 1)
                if has(2):
                    dve.wait_ge(res_added, (i - 1) * CT)
                    for j in range(CT):
                        a = acc[:, bass.ds((i - 2) * CT + j, 1), :].rearrange("p a t -> p (a t)")
                        dve.wait_ge(out_mm, (i - 2) * CT + j + 1)
                        nc.vector.scalar_tensor_tensor(a, ps_out[j][:], gates[:, 0:1], a, ALU.mult, ALU.add) \
                            .then_inc(acc_added, 1)
                    for j in range(CT):
                        a = acc[:, bass.ds((i - 2) * CT + j, 1), :].rearrange("p a t -> p (a t)")
                        wait_apart(dve, acc_added, (i - 2) * CT + j + 1)
                        nc.vector.bn_stats(st2[:, j], a).then_inc(st2_done, 1)
                    for j in range(CT):
                        wait_apart(dve, st2_done, (i - 2) * CT + j + 1)
                        nc.vector.bn_aggr(mv2[:, j], st2[:, j]).then_inc(mv2_done, 1)
                    dve.wait_ge(mv2_done, (i - 1) * CT)
                    if has(3):
                        dve.wait_ge(xn2_ready, (i - 2) * CT)
                    nc.vector.tensor_scalar(ve2[:], mv2[:, :, 1], LN_EPS, None, ALU.add).then_inc(ve2_ready, 1)
                    dve.wait_ge(rstd2_ready, i - 1)
                    nc.vector.scalar_tensor_tensor(nmr2[:], mv2[:, :, 0], -1.0, rstd2[:], ALU.mult, ALU.mult) \
                        .then_inc(nmr2_ready, 1)
                if has(3):
                    dve.wait_ge(router_mm, i - 2)
                    nc.vector.tensor_reduce(logits[:, bass.ds((i - 3) * CT, CT), :],
                                            ps_router.rearrange("p (a h e) -> p a e h", a=CT, h=2), AX.X,
                                            ALU.add).then_inc(logits_ready, 1)
                if at(i, 0):
                    dve.wait_ge(small_loaded, 16 * SMALL_LOADS)
                    router_weights()
                if at(i, 1):
                    weights_max(0, 0)
                if at(i, 2):
                    weights_scale(0, 0)
                if at(i, 3):
                    weights_low(0, 0, (0, 1))
                if at(i, NB):
                    weights_low(0, 0, (2,))

            turns(dve, turn)

            count = [0]

            def link(ins):
                count[0] += 1
                ins.then_inc(route_step, 1)
                dve.wait_ge(route_step, count[0])

            def per_token(n):
                return total[:, n, :].unsqueeze(2).broadcast_to([P, NT, E])

            Z, EXPZ, INH, DIST, W, FB, T1, T2, M1, M2 = range(10)
            pl = [plane[:, n] for n in range(10)]
            dve.wait_ge(logits_ready, NB)
            dve.wait_ge(const_ready, 3 + E)
            nc.vector.tensor_scalar(pl[Z], logits[:], unscale[:, ROUTER, 0:1], inv_temp[:], ALU.mult, ALU.mult) \
                .then_inc(route_z, 1)
            dve.wait_ge(route_exp, 1)
            link(nc.vector.tensor_scalar(pl[EXPZ], pl[EXPZ], 1.0, None, ALU.add))
            link(nc.vector.reciprocal(pl[INH], pl[EXPZ]))
            link(nc.vector.tensor_scalar(pl[T2], pl[INH], GOLDEN_CENTER, None, ALU.subtract))
            nc.vector.scalar_tensor_tensor(pl[DIST], pl[T2], -1.0, pl[T2], ALU.mult, ALU.max) \
                .then_inc(route_dist, 1)
            dve.wait_ge(route_z, 1)
            link(nc.vector.tensor_scalar(pl[T1], pl[Z], ZONE_LOW, None, ALU.is_ge))
            link(nc.vector.scalar_tensor_tensor(pl[T1], pl[Z], 0.0, pl[T1], ALU.is_le, ALU.mult))
            dve.wait_ge(route_exp, 3)
            link(nc.vector.tensor_tensor(pl[W], pl[W], pl[T1], ALU.mult))
            link(nc.vector.reduce_sum(total[:, 0, :], pl[W], AX.X))
            link(nc.vector.tensor_scalar(total[:, 0, :], total[:, 0, :], 1e-8, None, ALU.is_lt))
            link(nc.vector.tensor_copy(pl[T1], pl[FB]))
            for m in (M1, M2):
                link(nc.vector.tensor_reduce(total[:, 1, :], pl[T1], AX.X, ALU.max))
                link(nc.vector.tensor_tensor(pl[T2], pl[T1], per_token(1), ALU.is_ge))
                link(nc.vector.tensor_tensor(pl[T2], pl[T2], rank[:], ALU.mult))
                link(nc.vector.tensor_reduce(total[:, 2, :], pl[T2], AX.X, ALU.max))
                link(nc.vector.tensor_tensor(pl[m], pl[T2], per_token(2), ALU.is_equal))
                link(nc.vector.scalar_tensor_tensor(pl[T1], pl[m], -2.0, pl[T1], ALU.mult, ALU.add))
            link(nc.vector.tensor_tensor(pl[M1], pl[M1], pl[M2], ALU.add))
            link(nc.vector.tensor_tensor(pl[FB], pl[FB], pl[M1], ALU.mult))
            link(nc.vector.reduce_sum(total[:, 1, :], pl[FB], AX.X))
            link(nc.vector.tensor_scalar(total[:, 1, :], total[:, 1, :], 1e-8, None, ALU.max))
            link(nc.vector.reciprocal(total[:, 2, :], total[:, 1, :]))
            link(nc.vector.tensor_tensor(pl[FB], pl[FB], per_token(2), ALU.mult))
            link(nc.vector.tensor_tensor(pl[FB], pl[FB], per_token(0), ALU.mult))
            link(nc.vector.tensor_scalar(total[:, 3, :], total[:, 0, :], -1.0, 1.0, ALU.mult, ALU.add))
            link(nc.vector.tensor_tensor(pl[W], pl[W], per_token(3), ALU.mult))
            link(nc.vector.tensor_tensor(pl[W], pl[W], pl[FB], ALU.add))
            link(nc.vector.reduce_sum(total[:, 1, :], pl[W], AX.X))
            link(nc.vector.tensor_scalar(total[:, 1, :], total[:, 1, :], 1e-8, None, ALU.max))
            link(nc.vector.reciprocal(total[:, 2, :], total[:, 1, :]))
            link(nc.vector.tensor_scalar(total[:, 2, :], total[:, 2, :], gates[:, 1:2], None, ALU.mult))
            nc.vector.tensor_tensor(mix[:], pl[W], per_token(2), ALU.mult).then_inc(mix_ready, 1)
            dve.wait_ge(mix_ready, 1)

            def hidden(s, par):
                for f in range(KF):
                    if f == 0 and (not isinstance(s, int) or s >= 1):
                        dve.wait_ge(hh_ready, s)
                        dve.wait_ge(hl_ready, s)
                    dve.wait_ge(up_mm, s * KF + f + 1)
                    dve.wait_ge(silu_ready, s * KF + f + 1)
                    nc.vector.scalar_tensor_tensor(hbuf[:, f], ps_up[f % 2][:], unscale[:, WEIGHTS + par, 1:2],
                                                   silu[:, f % 2], ALU.mult, ALU.mult).then_inc(h_done, 1)
                    dve.wait_ge(h_done, s * KF + f + 1)
                    nc.vector.tensor_reduce(ham[:, f:f + 1], hbuf[:, f], AX.X, ALU.max,
                                            apply_absolute_value=True).then_inc(ham_done, 1)
                dve.wait_ge(ham_done, s * KF + KF)
                nc.vector.tensor_reduce(am[:, HIDDEN, 0:1], ham[:], AX.X, ALU.max).then_inc(h_am, 1)

            def hidden_split(s, hp):
                dve.wait_ge(h_am_all, s + 1)
                power_scale(HIDDEN + hp, 1, h_scaling, s, XSCALE).then_inc(h_scaled, 1)
                dve.wait_ge(h_scaled, s + 1)
                dve.wait_ge(hh_ready, s + 1)
                nc.vector.scalar_tensor_tensor(
                    hl[hp][:].rearrange("p k n -> p (k n)"), hbuf[:].rearrange("p k n -> p (k n)"),
                    scale[:, HIDDEN + hp, 0:1], hh[hp][:].rearrange("p k n -> p (k n)"), ALU.mult, ALU.subtract) \
                    .then_inc(hl_ready, 1)

            def combine(s, e, u):
                hp, par, blk = u % 2, u // NBLK % 2, u % NBLK
                ei = slice(e, e + 1) if isinstance(e, int) else bass.ds(e, 1)
                nc.vector.tensor_scalar(coef[:, hp], mix[:, blk * TPB:(blk + 1) * TPB, ei].rearrange("p a e -> p (a e)"),
                                        unscale[:, HIDDEN + hp, 0:1], unscale[:, WEIGHTS + par, 2:3], ALU.mult, ALU.mult) \
                    .then_inc(coef_ready, 1)
                dve.wait_ge(coef_ready, s + 1)
                for t in range(TPB):
                    dve.wait_ge(down_mm, s * TPB + t + 1)
                    a = acc[:, blk * TPB + t, :]
                    nc.vector.scalar_tensor_tensor(a, ps_down[t][:], coef[:, hp, t:t + 1], a, ALU.mult, ALU.add) \
                        .then_inc(combined, 1)

            def first():
                hidden(0, 0)
                hidden_split(0, 0)

            def step_turn(s, e, u, more):
                last = at(e, E - 1)
                local, other = u % NBLK, (u // NBLK + 1) % 2
                if more:
                    hidden(s + 1, (u + 1) // NBLK % 2)
                if local == 1 and not last:
                    weights_scale(e + 1, other)
                if more:
                    hidden_split(s + 1, (u + 1) % 2)
                combine(s, e, u)
                if local == 0 and not last:
                    weights_max(e + 1, other)
                if local == 1 and not last:
                    weights_low(e + 1, other)

            steps(dve, first, step_turn)

        @block.tensor
        def _(pe):
            pe.wait_ge(const_ready, 3)
            pe.wait_ge(proj_loaded, 16 * PROJ_LOADS)
            for n in range(2):
                for a in range(4):
                    last = nc.tensor.transpose(ps_tr[n][:, a * P:(a + 1) * P], proj_raw[:, 4 * n + a, :], ident[:])
                last.then_inc(projT_mm, 1)
            pe.wait_ge(projT_ready, 2)

            def turn(i, has):
                if has(0):
                    pe.wait_ge(in2_loaded, i * 16 + 16)
                    if has(1):
                        pe.wait_ge(exp_done, i * TT)
                    for k in range(CT):
                        last = nc.tensor.matmul(ps_theta[:], proj_w(0, k), in2[:, k], start=(k == 0), stop=(k == 1))
                    last.then_inc(theta_mm, 1)
                    pe.wait_ge(in1_ready, i * CT + CT)
                    for k in range(CT):
                        last = nc.tensor.matmul(ps_phi[:], proj_w(1, k), in1[:, k], start=(k == 0), stop=(k == 1))
                    last.then_inc(phi_mm, 1)
                if has(2):
                    pe.wait_ge(vh_ready, i - 1)
                    if has(4):
                        pe.wait_ge(logits_ready, i - 3)
                    nc.tensor.matmul(ps_var, mean_w[:], vh[:], start=True, stop=True).then_inc(var_mm, 1)
                if has(1):
                    for j in range(TT):
                        if j == 0:
                            pe.wait_ge(prob_ready, i * TT)
                        if j >= 2:
                            pe.wait_ge(probT_odd if j % 2 else probT_even, (i - 1) * 2 + j // 2)
                        for t in range(TT):
                            last = nc.tensor.transpose(ps_tr[j % 2][:, t * P:(t + 1) * P],
                                                       prob[:, t, j * P:(j + 1) * P], ident[:])
                        last.then_inc(probT_mm, 1)
                if has(0):
                    pe.wait_ge(theta_ready, i + 1)
                    pe.wait_ge(phi_ready, i + 1)
                    for j in range(TT):
                        if j < 2 and has(3):
                            pe.wait_ge(acc_added, (i - 2) * CT - j)
                        elif j == 0 and has(1):
                            pe.wait_ge(gx_ready, i)
                        nc.tensor.matmul(ps_score[j][:], thetaT[:, j * P:(j + 1) * P], phi[:], start=True,
                                         stop=True).then_inc(score_mm, 1)
                if has(1):
                    pe.wait_ge(gx_ready, i)
                    if has(2):
                        pe.wait_ge(tx_ready, i - 1)
                    for j in range(TT):
                        pe.wait_ge(probT_odd if j % 2 else probT_even, (i - 1) * 2 + j // 2 + 1)
                        last = nc.tensor.matmul(ps_tx[:], gx[:, j, :], probT[:, j], start=(j == 0), stop=(j == TT - 1))
                    last.then_inc(tx_mm, 1)
                if has(0):
                    pe.wait_ge(exp_done, i * TT + 1)
                    for j in range(TT):
                        for k in range(CT):
                            last = nc.tensor.matmul(ps_gx[:, j * P:(j + 1) * P], in1[:, k, j * P:(j + 1) * P],
                                                    proj_w(2, k), start=(k == 0), stop=(k == 1))
                    last.then_inc(gx_mm, 1)
                if has(3):
                    pe.wait_ge(xn2_ready, (i - 2) * CT)
                    for m in range(2):
                        if has(1):
                            pe.wait_ge(probT_odd if m else probT_even, i * 2)
                        for k in range(2):
                            for j in range(CT):
                                col = k * C + j * P
                                last = nc.tensor.transpose(ps_tr[m][:, col:col + P],
                                                           xn2[:, j, (2 * m + k) * P:(2 * m + k + 1) * P], ident[:])
                        last.then_inc(xT_mm, 1)
                if has(1):
                    pe.wait_ge(mvh_ready, i)
                    if has(2):
                        pe.wait_ge(veh_ready, i - 1)
                    nc.tensor.matmul(ps_mu, mean_w[:], mvh[:, 0:1], start=True, stop=True).then_inc(mu_mm, 1)
                if has(2):
                    pe.wait_ge(hid_ready, i - 1)
                    for j in range(CT):
                        if has(0) and j == 0:
                            pe.wait_ge(exp_done, i * TT + 2)
                        if has(0) and j == 1:
                            pe.wait_ge(gx_ready, i + 1)
                        if has(3):
                            pe.wait_ge(acc_added, (i - 3) * CT + j + 1)
                        nc.tensor.matmul(ps_out[j][:], out_wT(j), hid[:], start=True, stop=True).then_inc(out_mm, 1)
                if has(3):
                    pe.wait_ge(xl_ready, (i - 2) * 2)
                    if has(1):
                        pe.wait_ge(mu_read, i * 2 - 1)
                    elif has(2):
                        pe.wait_ge(veh_ready, i - 1)
                    else:
                        pe.wait_ge(logits_ready, i - 3)
                    pe.wait_ge(wrh_ready, 1)
                    pe.wait_ge(wrl_ready, 1)
                    for j in range(CT):
                        tok = bass.ds(((i - 3) * CT + j) * P, P)
                        o = ps_router[:, j * 2 * E:(j + 1) * 2 * E]
                        for k in range(KD):
                            w = wr2[:, k].rearrange("p h e -> p (h e)")
                            nc.tensor.matmul(o, xh[:, k, tok], w, start=(k == 0), stop=False)
                            last = nc.tensor.matmul(o, xl[:, k, tok], w, start=False, stop=(k == KD - 1))
                    last.then_inc(router_mm, 1)

            def out_wT(j):
                return projT[:, 6 + j, :]

            def gate_up(s, e, blk, par, tiles=range(KF)):
                tok = slice(blk * TB, (blk + 1) * TB)
                if blk == 0:
                    pe.wait_ge(wh_ready, e * 3 + 3)
                    pe.wait_ge(wl_ready, e * 3 + 3)
                for f in tiles:
                    cols = slice(f * P, (f + 1) * P)
                    for w, ps, done, used in ((0, ps_gate, gate_mm, silu_ready), (1, ps_up, up_mm, h_done)):
                        if not isinstance(s, int) or s * KF + f >= 2:
                            pe.wait_ge(used, s * KF + f - 1)
                        for k in range(KD):
                            a, b = wh[par][:, w, k, cols], wl[par][:, w, k, cols]
                            nc.tensor.matmul(ps[f % 2][:], a, xh[:, k, tok], start=(k == 0), stop=False)
                            nc.tensor.matmul(ps[f % 2][:], a, xl[:, k, tok], start=False, stop=False)
                            last = nc.tensor.matmul(ps[f % 2][:], b, xh[:, k, tok], start=False, stop=(k == KD - 1))
                        last.then_inc(done, 1)

            def down(s, hp, par):
                if at(s, STEPS - 1):
                    pe.wait_ge(combined, s * TPB)
                pe.wait_ge(hh_ready, s + 1)
                pe.wait_ge(hl_ready, s + 1)
                for t in range(TPB):
                    rows = slice(t * P, (t + 1) * P)
                    for k in range(KF):
                        a, b = hh[hp][:, k, rows], hl[hp][:, k, rows]
                        nc.tensor.matmul(ps_down[t][:], a, wh[par][:, 2, k, :], start=(k == 0), stop=False)
                        nc.tensor.matmul(ps_down[t][:], a, wl[par][:, 2, k, :], start=False, stop=False)
                        last = nc.tensor.matmul(ps_down[t][:], b, wh[par][:, 2, k, :], start=False,
                                                stop=(k == KF - 1))
                    last.then_inc(down_mm, 1)

            def step_turn(s, e, u, more):
                if more:
                    n = u + 1
                    gate_up(s + 1, e + (1 if n % NBLK == 0 else 0), n % NBLK, n // NBLK % 2)
                down(s, u % 2, u // NBLK % 2)

            def after(i):
                if at(i, NB):
                    pe.wait_ge(exp_done, NB * TT)
                    gate_up(0, 0, 0, 0, range(0, 1))
                if at(i, NB + 1):
                    pe.wait_ge(acc_added, NB * CT)
                    gate_up(0, 0, 0, 0, range(1, 2))

            turns(pe, turn, after)
            steps(pe, lambda: gate_up(0, 0, 0, 0, range(2, KF)), step_turn)


_INS = ['x', 'ctx_2048', 'g_xattn', 'g_ffn', 'L0_xattn_theta_w', 'L0_xattn_theta_b', 'L0_xattn_phi_w',
        'L0_xattn_phi_b', 'L0_xattn_g_w', 'L0_xattn_g_b', 'L0_xattn_ln_gamma', 'L0_xattn_ln_beta',
        'L0_xattn_out_w', 'L0_xattn_out_b', 'L0_ffn_Wg', 'L0_ffn_Wu', 'L0_ffn_Wd', 'L0_ffn_Wr',
        'L0_ffn_temperature']


def kernel(**inputs):
    import numpy as _np
    import concourse.bacc as _bacc
    from concourse.bass_utils import run_bass_kernel_spmd as _run

    nc = _bacc.Bacc("TRN2", target_bir_lowering=False, num_devices=1)
    arrays, args = {}, []
    for name in _INS:
        a = _np.ascontiguousarray(inputs[name])
        arrays[f"in_{name}_dram"] = a
        args.append(nc.dram_tensor(f"in_{name}_dram", a.shape, mybir.dt.from_np(a.dtype), kind="ExternalInput").ap())
    args.append(nc.dram_tensor("out_0_dram", inputs['x'].shape, F32, kind="ExternalOutput").ap())
    build(nc, *args)
    r = _run(nc, [arrays], core_ids=[0])
    return r.results[0]["out_0_dram"]
```

```python
import math
from contextlib import ExitStack

import concourse.bass as bass
from concourse import mybir

F32 = mybir.dt.float32
F16 = mybir.dt.float16
U32 = mybir.dt.uint32
ALU = mybir.AluOpType
ACT = mybir.ActivationFunctionType
AX = mybir.AxisListType
ABSMAX = bass.bass_isa.ReduceOp.absmax

P = 128
LN_EPS = 1e-5
GOLDEN_CENTER = 1.0 / math.e
GOLDEN_LOWER = 0.5 - math.log(4.0 / 3.0)
ZONE_LOW = math.log(GOLDEN_LOWER / (1.0 - GOLDEN_LOWER))
EXPONENT_BITS = 0x7F800000
XSCALE = 1024.0
TOP = 2.0 ** 14
TINY = 2.0 ** -100


def build(nc, x, ctx_in, g_xattn, g_ffn, theta_w, theta_b, phi_w, phi_b, g_w, g_b, ln_gamma, ln_beta,
          out_w, out_b, Wg, Wu, Wd, Wr, temperature, out):
    NB, C, T = x.shape
    L = theta_w.shape[0]
    E, D, F = Wg.shape
    CT = C // P
    TT = T // P
    KD = D // P
    KF = F // P
    NT = NB * CT
    TB = 512
    TPB = TB // P
    NBLK = NB * C // TB
    STEPS = E * NBLK
    PAIR = 2 * NBLK
    assert L == P and T == 512 and D == T and CT == 2 and NBLK == 4

    x_v = x.rearrange("b (j p) t -> b p j t", p=P)
    ctx_v = ctx_in.rearrange("b (j p) t -> b p j t", p=P)
    out_v = out.rearrange("b (j p) t -> p (b j) t", p=P)
    w_v = [w.rearrange("e (k p) n -> e p k n", p=P) for w in (Wg, Wu, Wd)]

    with ExitStack() as stack:
        def sb(name, shape, dt=F32):
            return stack.enter_context(nc.sbuf_tensor(name, shape, dt))

        def sem(name):
            return stack.enter_context(nc.semaphore(name))

        bank = [stack.enter_context(nc.psum_tensor(f"bank{i}", [P, 512], F32)) for i in range(8)]

        acc = sb("acc", [P, NT, T])
        xh = sb("xh", [P, KD, NB * C], F16)
        xl = sb("xl", [P, KD, NB * C], F16)
        ident = sb("ident", [P, P])
        mean_w = sb("mean_w", [P, P])
        neg_half = sb("neg_half", [P, 2])
        gate_raw = sb("gate_raw", [P, 3])
        gates = sb("gates", [P, 2])
        inv_temp = sb("inv_temp", [P, 1])
        logits = sb("logits", [P, NT, E])
        mix = sb("mix", [P, NT, E])

        wh1 = sb("wh1", [P, 3, KD, F], F16)
        wl1 = sb("wl1", [P, 3, KD, F], F16)

        def borrowed(of, w, tiles):
            return of[:, w:w + tiles // 2].rearrange("p w k n -> p (w k n)").bitcast(F32) \
                .rearrange("p (j t) -> p j t", t=T)

        prob = borrowed(wh1, 0, TT)
        in2 = borrowed(wh1, 2, CT)
        probT = borrowed(wl1, 0, TT)
        in1 = borrowed(wl1, 2, CT)
        res = sb("res", [P, CT, T])
        thetaT = sb("thetaT", [P, T])
        phi = sb("phi", [P, T])
        gx = sb("gx", [P, TT, L])
        tx = sb("tx", [P, T])
        z = sb("z", [P, T])
        hid = sb("hid", [P, T])
        xn2 = sb("xn2", [P, CT, T])
        gamma = sb("gamma", [P, T])
        beta = sb("beta", [P, T])
        proj_raw = sb("proj_raw", [P, 8, P])
        projT = sb("projT", [P, 8, P])
        theta_bc = sb("theta_bc", [P, 1])
        phi_bc = sb("phi_bc", [P, 1])
        g_bc = sb("g_bc", [P, 1])
        out_bc = sb("out_bc", [P, CT])
        st1 = sb("st1", [P, CT, 6])
        mv1 = sb("mv1", [P, CT, 2])
        ve1 = sb("ve1", [P, CT])
        rstd1 = sb("rstd1", [P, CT])
        st2 = sb("st2", [P, CT, 6])
        mv2 = sb("mv2", [P, CT, 2])
        ve2 = sb("ve2", [P, CT])
        rstd2 = sb("rstd2", [P, CT])
        nmr2 = sb("nmr2", [P, CT])
        sth = sb("sth", [P, 6])
        mvh = sb("mvh", [P, 2])
        muh = sb("muh", [P, 1])
        dh = sb("dh", [P, 1])
        vh = sb("vh", [P, 1])
        veh = sb("veh", [P, 1])
        rstdh = sb("rstdh", [P, 1])
        nmax = sb("nmax", [P, TT])
        rsum = sb("rsum", [P, TT])
        rinv = sb("rinv", [P, TT])
        wr_raw = sb("wr_raw", [P, KD, E])
        wr2 = sb("wr2", [P, KD, 2, E], F16)
        wrh, wrl = wr2[:, :, 0, :], wr2[:, :, 1, :]

        plane = sb("plane", [P, 10, NT, E])
        total = sb("total", [P, 6, NT])
        rank = sb("rank", [P, NT, E])

        wraw = sb("wraw", [P, 3, KD, F])
        wh = [sb("wh0", [P, 3, KD, F], F16), wh1]
        wl = [sb("wl0", [P, 3, KD, F], F16), wl1]
        silu = sb("silu", [P, 2, TB])
        hbuf = sb("hbuf", [P, KF, TB])
        hh = [sb(f"hh{i}", [P, KF, TB], F16) for i in range(2)]
        hl = [sb(f"hl{i}", [P, KF, TB], F16) for i in range(2)]
        ROUTER, WEIGHTS, HIDDEN = 0, 1, 3
        am = sb("am", [P, 5, 3])
        am_all = sb("am_all", [P, 5, 3])
        pow2 = sb("pow2", [P, 5, 3])
        scale = sb("scale", [P, 5, 3])
        unscale = sb("unscale", [P, 5, 3])
        ham = sb("ham", [P, KF])
        coef = sb("coef", [P, 2, TPB])

        ps_theta, ps_phi = bank[0], bank[1]
        ps_gx = bank[2]
        ps_out = [bank[3], bank[2]]
        ps_score = [bank[2], bank[3], bank[0], bank[1]]
        ps_tr = [bank[4], bank[5]]
        ps_tx = bank[6]
        ps_mu = bank[7][:, 0:1]
        ps_var = bank[7][:, 1:2]
        ps_router = bank[7][:, 16:16 + CT * 2 * E]
        ps_gate = [bank[0], bank[2]]
        ps_up = [bank[1], bank[3]]
        ps_down = [bank[4], bank[5], bank[6], bank[7]]

        const_ready = sem("const_ready")
        waits_met = sem("waits_met")
        ident_zero = sem("ident_zero")
        proj_loaded = sem("proj_loaded")
        proj2_loaded = sem("proj2_loaded")
        gates_loaded = sem("gates_loaded")
        bias_loaded = sem("bias_loaded")
        small_loaded = sem("small_loaded")
        gates_ready = sem("gates_ready")
        temp_ready = sem("temp_ready")
        projT_mm = sem("projT_mm")
        projT_ready = sem("projT_ready")
        wr_scaling = sem("wr_scaling")
        w_scaling = sem("w_scaling")
        h_scaling = sem("h_scaling")
        x_loaded = sem("x_loaded")
        in2_loaded = sem("in2_loaded")
        st1_done = sem("st1_done")
        mv1_done = sem("mv1_done")
        ve1_ready = sem("ve1_ready")
        rstd1_ready = sem("rstd1_ready")
        in1_ready = sem("in1_ready")
        res_ready = sem("res_ready")
        res_added = sem("res_added")
        theta_mm = sem("theta_mm")
        phi_mm = sem("phi_mm")
        theta_ready = sem("theta_ready")
        phi_ready = sem("phi_ready")
        score_mm = sem("score_mm")
        rowmax_ready = sem("rowmax_ready")
        exp_done = sem("exp_done")
        rinv_ready = sem("rinv_ready")
        prob_ready = sem("prob_ready")
        probT_mm = sem("probT_mm")
        probT_even = sem("probT_even")
        probT_odd = sem("probT_odd")
        gx_mm = sem("gx_mm")
        gx_ready = sem("gx_ready")
        tx_mm = sem("tx_mm")
        tx_ready = sem("tx_ready")
        sth_done = sem("sth_done")
        mvh_ready = sem("mvh_ready")
        mu_mm = sem("mu_mm")
        mu_read = sem("mu_read")
        vh_ready = sem("vh_ready")
        var_mm = sem("var_mm")
        veh_ready = sem("veh_ready")
        rstdh_ready = sem("rstdh_ready")
        z1_done = sem("z1_done")
        z2_done = sem("z2_done")
        hid_ready = sem("hid_ready")
        out_mm = sem("out_mm")
        acc_added = sem("acc_added")
        st2_done = sem("st2_done")
        mv2_done = sem("mv2_done")
        ve2_ready = sem("ve2_ready")
        rstd2_ready = sem("rstd2_ready")
        nmr2_ready = sem("nmr2_ready")
        xn2_ready = sem("xn2_ready")
        xT_mm = sem("xT_mm")
        xh_ready = sem("xh_ready")
        xl_ready = sem("xl_ready")
        router_mm = sem("router_mm")
        logits_ready = sem("logits_ready")
        wr_am = sem("wr_am")
        wr_am_all = sem("wr_am_all")
        wr_scaled = sem("wr_scaled")
        wrh_ready = sem("wrh_ready")
        wrl_ready = sem("wrl_ready")
        route_z = sem("route_z")
        route_exp = sem("route_exp")
        route_step = sem("route_step")
        route_dist = sem("route_dist")
        mix_ready = sem("mix_ready")
        w_loaded = [sem(f"{name}_loaded") for name in ("wg", "wu", "wd")]
        w_am = sem("w_am")
        w_am_all = sem("w_am_all")
        w_scaled = sem("w_scaled")
        wh_ready = sem("wh_ready")
        wl_ready = sem("wl_ready")
        raw_scaled = sem("raw_scaled")
        gate_mm = sem("gate_mm")
        up_mm = sem("up_mm")
        silu_ready = sem("silu_ready")
        h_done = sem("h_done")
        ham_done = sem("ham_done")
        h_am = sem("h_am")
        h_am_all = sem("h_am_all")
        h_scaled = sem("h_scaled")
        hh_ready = sem("hh_ready")
        hl_ready = sem("hl_ready")
        down_mm = sem("down_mm")
        coef_ready = sem("coef_ready")
        combined = sem("combined")
        stored = sem("stored")

        BIAS_LOADS, GATES_LOADS, SMALL_LOADS = 3, 3, 5

        def at(i, turn):
            return isinstance(i, int) and i == turn

        def wait_apart(eng, signal, value):
            eng.wait_ge(signal, value)
            eng.sem_inc(waits_met, 1)

        block = stack.enter_context(nc.Block())

        LOOP_FROM, LOOP_TO, LAST_TURN = 4, NB - 1, NB + 2

        def turns(eng, turn, after=lambda i: None):
            for i in range(-1, LOOP_FROM):
                turn(i, lambda k, i=i: 0 <= i - k < NB)
            with eng.Fori(LOOP_FROM, LOOP_TO) as i:
                turn(i, lambda k: True)
            for i in range(LOOP_TO, LAST_TURN + 1):
                turn(i, lambda k, i=i: 0 <= i - k < NB)
                after(i)

        def steps(eng, first, turn, done=0):
            first()
            with eng.Fori(0, E // 2 - 1) as m:
                for u in range(done, done + PAIR):
                    turn(m * PAIR + u, m * 2 + u // NBLK, u % PAIR, True)
            m = E // 2 - 1
            for u in range(done, PAIR):
                turn(m * PAIR + u, m * 2 + u // NBLK, u, u < PAIR - 1)

        @block.sync
        def _(sp):
            def load_x(b):
                if not isinstance(b, int) or b >= 1:
                    wait_apart(sp, x_loaded, b * 16)
                sp.dma_start(acc[:, bass.ds(b * CT, CT), :], x_v[b]).then_inc(x_loaded, 16)

            def load_in2(b):
                wait_apart(sp, theta_mm, b)
                wait_apart(sp, res_ready, b * CT)
                sp.dma_start(in2[:, :, :], ctx_v[b]).then_inc(in2_loaded, 16)

            sp.dma_start(proj_raw[:, 0:2, :], theta_w.rearrange("l (k p) -> l k p", p=P)).then_inc(proj_loaded, 16)
            sp.dma_start(proj_raw[:, 2:4, :], phi_w.rearrange("l (k p) -> l k p", p=P)).then_inc(proj_loaded, 16)
            load_x(0)
            sp.dma_start(proj_raw[:, 4:6, :], g_w.rearrange("l (k p) -> l k p", p=P)).then_inc(proj2_loaded, 16)
            sp.dma_start(proj_raw[:, 6:8, :], out_w.rearrange("(k p) l -> p k l", p=P)).then_inc(proj2_loaded, 16)
            sp.dma_start(wr_raw[:], Wr.rearrange("(k p) e -> p k e", p=P)).then_inc(small_loaded, 16)
            for j in range(CT):
                sp.dma_start(out_bc[:, j:j + 1], out_b[j * P:(j + 1) * P].rearrange("(l a) -> l a", a=1)) \
                    .then_inc(small_loaded, 16)
            sp.dma_start(gamma[:], ln_gamma).then_inc(small_loaded, 16)
            sp.dma_start(beta[:], ln_beta).then_inc(small_loaded, 16)
            load_x(1)
            load_in2(1)
            load_x(2)
            for i in range(3):
                sp.dma_start(wraw[:, i], w_v[i][0]).then_inc(w_loaded[i], 16)

            with sp.Fori(2, NB - 1) as b:
                load_in2(b)
                load_x(b + 1)
            load_in2(NB - 1)

            with sp.Fori(1, E) as e:
                sp.wait_ge(wh_ready, e * 3)
                wait_apart(sp, wl_ready, e * 3)
                for i in range(3):
                    sp.dma_start(wraw[:, i], w_v[i][e]).then_inc(w_loaded[i], 16)

            for blk in range(NBLK):
                for t in range(TPB):
                    sp.wait_ge(combined, (STEPS - NBLK + blk) * TPB + t + 1)
                    n = blk * TPB + t
                    sp.dma_start(out_v[:, n, :], acc[:, n, :]).then_inc(stored, 16)
            sp.wait_ge(stored, 16 * NT)

        @block.gpsimd
        def _(pool):
            nc.gpsimd.memset(ident[:], 0.0).then_inc(ident_zero, 1)
            nc.gpsimd.memset(mean_w[:], 1.0 / P).then_inc(const_ready, 1)
            nc.gpsimd.memset(neg_half[:], -0.5).then_inc(const_ready, 1)
            pool.wait_ge(ident_zero, 1)
            nc.gpsimd.affine_select(out=ident[:], in_=ident[:], compare_op=ALU.not_equal, fill=1.0, base=0,
                                    pattern=[[-1, P]], channel_multiplier=1).then_inc(const_ready, 1)
            for e in range(E):
                nc.gpsimd.memset(rank[:, :, e], float(E - e)).then_inc(const_ready, 1)
            pool.wait_ge(const_ready, 3)

            def turn(i, has):
                if has(2):
                    pool.wait_ge(veh_ready, i - 2 + 1)
                    nc.gpsimd.tensor_tensor(rstdh[:], veh[:], neg_half[:, 0:1], ALU.pow).then_inc(rstdh_ready, 1)
                if has(0):
                    if at(i, 0):
                        pool.wait_ge(wr_am, 1)
                        nc.gpsimd.partition_all_reduce(am_all[:, ROUTER, 0:1], am[:, ROUTER, 0:1], P, ABSMAX) \
                            .then_inc(wr_am_all, 1)
                        pool.wait_ge(gates_ready, 1)
                        pool.wait_ge(small_loaded, 16 * SMALL_LOADS)
                    if has(1):
                        wait_apart(pool, res_added, i * CT)
                    wait_apart(pool, in2_loaded, i * 16 + 16)
                    for j in range(CT):
                        nc.gpsimd.tensor_scalar(res[:, j], in2[:, j], out_bc[:, j:j + 1], gates[:, 0:1],
                                                ALU.add, ALU.mult).then_inc(res_ready, 1)
                    pool.wait_ge(in1_ready, i * CT + CT)
                    for j in range(CT):
                        pool.wait_ge(res_ready, i * CT + j + 1)
                        a = acc[:, bass.ds(i * CT + j, 1), :].rearrange("p a t -> p (a t)")
                        nc.gpsimd.tensor_tensor(a, a, res[:, j], ALU.add).then_inc(res_added, 1)
                if has(-1):
                    pool.wait_ge(ve1_ready, i + 2)
                    nc.gpsimd.tensor_tensor(rstd1[:], ve1[:], neg_half[:], ALU.pow).then_inc(rstd1_ready, 1)
                if at(i, LOOP_TO):
                    first_weights_low(0)
                    first_weights_low(1)
                if has(2):
                    pool.wait_ge(ve2_ready, i - 2 + 1)
                    nc.gpsimd.tensor_tensor(rstd2[:], ve2[:], neg_half[:], ALU.pow).then_inc(rstd2_ready, 1)
                if at(i, 2):
                    all_reduce_weights(0, 0)

            def first_weights_low(w):
                pool.wait_ge(wh_ready, w + 1)
                nc.gpsimd.tensor_tensor(wl[0][:, w].rearrange("p k n -> p (k n)"),
                                        wraw[:, w].rearrange("p k n -> p (k n)"),
                                        wh[0][:, w].rearrange("p k n -> p (k n)"), ALU.subtract) \
                    .then_inc(wl_ready, 1)

            def all_reduce_weights(e, par):
                wait_apart(pool, w_am, e * 3 + 3)
                nc.gpsimd.partition_all_reduce(am_all[:, WEIGHTS + par, :], am[:, WEIGHTS + par, :], P, ABSMAX) \
                    .then_inc(w_am_all, 1)

            def all_reduce_hidden(s, hp):
                wait_apart(pool, h_am, s + 1)
                nc.gpsimd.partition_all_reduce(am_all[:, HIDDEN + hp, 0:1], am[:, HIDDEN, 0:1], P, ABSMAX) \
                    .then_inc(h_am_all, 1)

            def step_turn(s, e, u, more):
                if more:
                    all_reduce_hidden(s + 1, (u + 1) % 2)
                if u % NBLK == 0 and not at(e, E - 1):
                    all_reduce_weights(e + 1, (u // NBLK + 1) % 2)

            turns(pool, turn)
            first_weights_low(2)
            steps(pool, lambda: all_reduce_hidden(0, 0), step_turn)

        def proj_w(which, k):
            return projT[:, 2 * which + k, :]

        @block.scalar
        def _(act):
            act.dma_start(in2[:, :, :], ctx_v[0]).then_inc(in2_loaded, 16)
            for dst, src in ((gate_raw[:, 0:1], g_xattn), (gate_raw[:, 1:2], g_ffn), (gate_raw[:, 2:3], temperature)):
                act.dma_start(dst, src.partition_broadcast(P)).then_inc(gates_loaded, 16)
            act.dma_start(theta_bc[:], theta_b.rearrange("(l a) -> l a", a=1)).then_inc(bias_loaded, 16)
            act.dma_start(phi_bc[:], phi_b.rearrange("(l a) -> l a", a=1)).then_inc(bias_loaded, 16)
            act.dma_start(g_bc[:], g_b.rearrange("(l a) -> l a", a=1)).then_inc(bias_loaded, 16)
            act.wait_ge(gates_loaded, 16 * GATES_LOADS)
            nc.scalar.activation(gates[:], gate_raw[:, 0:2], ACT.Tanh).then_inc(gates_ready, 1)

            def copy_probT(i, j, has):
                act.wait_ge(probT_mm, (i - 1) * TT + j + 1)
                if has(2):
                    act.wait_ge(tx_mm, i - 1)
                nc.scalar.copy(probT[:, j], ps_tr[j % 2][:]).then_inc(probT_even, 1)

            def turn(i, has):
                if has(0):
                    act.wait_ge(theta_mm, i + 1)
                    if has(1):
                        act.wait_ge(score_mm, i * TT)
                    nc.scalar.activation(thetaT[:], ps_theta[:], ACT.Identity, bias=theta_bc[:]) \
                        .then_inc(theta_ready, 1)
                    act.wait_ge(phi_mm, i + 1)
                    nc.scalar.activation(phi[:], ps_phi[:], ACT.Identity, bias=phi_bc[:]).then_inc(phi_ready, 1)
                if at(i, 0):
                    act.wait_ge(projT_mm, 2)
                    nc.scalar.copy(projT[:, 4:8, :].rearrange("p a l -> p (a l)"), ps_tr[1][:]).then_inc(projT_ready, 1)
                    act.wait_ge(small_loaded, 16 * SMALL_LOADS)
                    act.wait_ge(wr_scaled, 1)
                    nc.scalar.activation(wrh, wr_raw[:], ACT.Copy, scale=scale[:, ROUTER, 0:1]) \
                        .then_inc(wrh_ready, 1)
                if has(1):
                    copy_probT(i, 0, has)
                if has(3):
                    act.wait_ge(nmr2_ready, i - 2)
                    for j in range(CT):
                        a = acc[:, bass.ds((i - 3) * CT + j, 1), :].rearrange("p a t -> p (a t)")
                        nc.scalar.activation(xn2[:, j], a, ACT.Identity, bias=nmr2[:, j:j + 1],
                                             scale=rstd2[:, j:j + 1]).then_inc(xn2_ready, 1)
                if has(1):
                    copy_probT(i, 2, has)
                if has(0):
                    if has(1):
                        act.wait_ge(probT_mm, i * TT)
                        act.wait_ge(rinv_ready, i)
                    for j in range(TT):
                        act.wait_ge(rowmax_ready, i * TT + j + 1)
                        nc.scalar.activation(prob[:, j], ps_score[j][:], ACT.Exp, bias=nmax[:, j:j + 1],
                                             accum_out=rsum[:, j:j + 1]).then_inc(exp_done, 1)
                if has(2):
                    act.wait_ge(z2_done, i - 1)
                    if has(3):
                        act.wait_ge(out_mm, (i - 2) * CT)
                    nc.scalar.activation(hid[:], z[:], ACT.Relu).then_inc(hid_ready, 1)
                if at(i, 3):
                    first_weights_scaled(0)
                if at(i, LOOP_TO):
                    first_weights_high(1)
                if has(1):
                    act.wait_ge(tx_mm, i)
                    if has(2):
                        act.wait_ge(z1_done, i - 1)
                    nc.scalar.activation(tx[:], ps_tx[:], ACT.Identity, bias=g_bc[:]).then_inc(tx_ready, 1)
                if has(0):
                    act.wait_ge(gx_mm, i + 1)
                    if has(1):
                        act.wait_ge(tx_mm, i)
                    nc.scalar.copy(gx[:].rearrange("p a l -> p (a l)"), ps_gx[:]).then_inc(gx_ready, 1)
                if has(3):
                    for m in range(2):
                        act.wait_ge(xT_mm, (i - 3) * 2 + m + 1)
                        nc.scalar.activation(
                            xh[:, 2 * m:2 * m + 2, bass.ds((i - 3) * C, C)],
                            ps_tr[m][:].rearrange("p (k c) -> p k c", k=2), ACT.Copy, scale=XSCALE) \
                            .then_inc(xh_ready, 1)
                if at(i, 3):
                    first_weights_high(0)
                    first_weights_scaled(1)

            def weights_high(e, par, w):
                act.wait_ge(w_scaled, e + 1)
                nc.scalar.activation(wh[par][:, w], wraw[:, w], ACT.Copy, scale=scale[:, WEIGHTS + par, w:w + 1]) \
                    .then_inc(wh_ready, 1)

            def silu_of(s, par, f):
                act.wait_ge(gate_mm, s * KF + f + 1)
                if not isinstance(s, int) or s * KF + f >= 2:
                    act.wait_ge(h_done, s * KF + f - 1)
                nc.scalar.activation(silu[:, f % 2], ps_gate[f % 2][:], ACT.Silu,
                                     scale=unscale[:, WEIGHTS + par, 0:1]).then_inc(silu_ready, 1)

            def first_weights_scaled(w):
                act.wait_ge(w_scaled, 1)
                nc.scalar.activation(wraw[:, w], wraw[:, w], ACT.Copy, scale=scale[:, WEIGHTS, w:w + 1]) \
                    .then_inc(raw_scaled, 1)

            def first_weights_high(w):
                act.wait_ge(raw_scaled, w + 1)
                nc.scalar.copy(wh[0][:, w], wraw[:, w]).then_inc(wh_ready, 1)

            def after(i):
                if at(i, NB):
                    silu_of(0, 0, 0)
                    first_weights_scaled(2)
                    silu_of(0, 0, 1)
                if at(i, NB + 1):
                    first_weights_high(2)
                    silu_of(0, 0, 2)

            act.wait_ge(bias_loaded, 16 * BIAS_LOADS)
            turns(act, turn, after)

            act.wait_ge(route_z, 1)
            nc.scalar.activation(plane[:, 1], plane[:, 0], ACT.Exp, scale=-1.0).then_inc(route_exp, 1)
            act.wait_ge(route_dist, 1)
            nc.scalar.activation(plane[:, 4], plane[:, 3], ACT.Exp, scale=-1.0 / 0.1).then_inc(route_exp, 1)
            nc.scalar.activation(plane[:, 5], plane[:, 3], ACT.Exp, scale=-1.0 / 0.3).then_inc(route_exp, 1)

            def hidden_high(s, hp):
                act.wait_ge(h_scaled, s + 1)
                nc.scalar.activation(hh[hp][:], hbuf[:], ACT.Copy, scale=scale[:, HIDDEN + hp, 0:1]) \
                    .then_inc(hh_ready, 1)

            def step_turn(s, e, u, more):
                last = at(e, E - 1)
                if more:
                    for f in range(KF):
                        silu_of(s + 1, (u + 1) // NBLK % 2, f)
                    hidden_high(s + 1, (u + 1) % 2)
                if u % NBLK == 1 and not last:
                    act.wait_ge(gate_mm, s * KF + KF)
                    for w in range(3):
                        weights_high(e + 1, (u // NBLK + 1) % 2, w)

            steps(act, lambda: (silu_of(0, 0, 3), hidden_high(0, 0)), step_turn)

        @block.vector
        def _(dve):
            def power_scale(slot, n, scaling, turn, extra):
                sl, seen = slice(0, n), turn * 4
                nc.vector.tensor_scalar(am_all[:, slot, sl], am_all[:, slot, sl], TINY, None, ALU.max) \
                    .then_inc(scaling, 1)
                dve.wait_ge(scaling, seen + 1)
                nc.vector.tensor_scalar(pow2[:, slot, sl].bitcast(U32), am_all[:, slot, sl].bitcast(U32),
                                        EXPONENT_BITS, None, ALU.bitwise_and).then_inc(scaling, 1)
                dve.wait_ge(scaling, seen + 2)
                nc.vector.reciprocal(scale[:, slot, sl], pow2[:, slot, sl]).then_inc(scaling, 1)
                nc.vector.tensor_scalar(unscale[:, slot, sl], pow2[:, slot, sl], extra / TOP, None, ALU.mult) \
                    .then_inc(scaling, 1)
                dve.wait_ge(scaling, seen + 4)
                return nc.vector.tensor_scalar(scale[:, slot, sl], scale[:, slot, sl], TOP, None, ALU.mult)

            def router_weights_high():
                nc.vector.reciprocal(inv_temp[:], gate_raw[:, 2:3]).then_inc(temp_ready, 1)
                nc.vector.tensor_reduce(am[:, 0, 0:1], wr_raw[:].rearrange("p k e -> p (k e)"), AX.X, ALU.max,
                                        apply_absolute_value=True).then_inc(wr_am, 1)
                dve.wait_ge(wr_am_all, 1)
                power_scale(ROUTER, 1, wr_scaling, 0, 1.0 / XSCALE).then_inc(wr_scaled, 1)

            def router_weights_low():
                dve.wait_ge(wr_scaled, 1)
                dve.wait_ge(wrh_ready, 1)
                nc.vector.scalar_tensor_tensor(wrl, wr_raw[:], scale[:, ROUTER, 0:1], wrh, ALU.mult,
                                               ALU.subtract).then_inc(wrl_ready, 1)

            def weights_max(e, par, which=(0, 1, 2)):
                for w in which:
                    dve.wait_ge(w_loaded[w], e * 16 + 16)
                    nc.vector.tensor_reduce(am[:, WEIGHTS + par, w:w + 1], wraw[:, w].rearrange("p k n -> p (k n)"),
                                            AX.X, ALU.max, apply_absolute_value=True).then_inc(w_am, 1)

            def weights_scale(e, par):
                dve.wait_ge(w_am_all, e + 1)
                power_scale(WEIGHTS + par, 3, w_scaling, e, 1.0 / XSCALE).then_inc(w_scaled, 1)

            def weights_low(e, par):
                dve.wait_ge(w_scaled, e + 1)
                for w in range(3):
                    dve.wait_ge(wh_ready, e * 3 + w + 1)
                    nc.vector.scalar_tensor_tensor(
                        wl[par][:, w].rearrange("p k n -> p (k n)"), wraw[:, w].rearrange("p k n -> p (k n)"),
                        scale[:, WEIGHTS + par, w:w + 1], wh[par][:, w].rearrange("p k n -> p (k n)"),
                        ALU.mult, ALU.subtract).then_inc(wl_ready, 1)

            def hidden(s, par, f):
                if f == 0 and (not isinstance(s, int) or s >= 1):
                    dve.wait_ge(hh_ready, s)
                    dve.wait_ge(hl_ready, s)
                dve.wait_ge(up_mm, s * KF + f + 1)
                dve.wait_ge(silu_ready, s * KF + f + 1)
                nc.vector.scalar_tensor_tensor(hbuf[:, f], ps_up[f % 2][:], unscale[:, WEIGHTS + par, 1:2],
                                               silu[:, f % 2], ALU.mult, ALU.mult).then_inc(h_done, 1)
                dve.wait_ge(h_done, s * KF + f + 1)
                nc.vector.tensor_reduce(ham[:, f:f + 1], hbuf[:, f], AX.X, ALU.max,
                                        apply_absolute_value=True).then_inc(ham_done, 1)
                if f == KF - 1:
                    dve.wait_ge(ham_done, s * KF + KF)
                    nc.vector.tensor_reduce(am[:, HIDDEN, 0:1], ham[:], AX.X, ALU.max).then_inc(h_am, 1)

            def after(i):
                if at(i, NB):
                    hidden(0, 0, 0)

            def copy_probT(i, j, has):
                dve.wait_ge(probT_mm, (i - 1) * TT + j + 1)
                if has(2):
                    dve.wait_ge(tx_mm, i - 1)
                nc.vector.tensor_copy(probT[:, j], ps_tr[j % 2][:]).then_inc(probT_odd, 1)

            def row_maximum(i, j):
                dve.wait_ge(score_mm, i * TT + j + 1)
                nc.vector.tensor_reduce(nmax[:, j:j + 1], ps_score[j][:], AX.X, ALU.max,
                                        negate=True).then_inc(rowmax_ready, 1)

            def read_logits(i):
                dve.wait_ge(router_mm, i - 3)
                nc.vector.tensor_reduce(logits[:, bass.ds((i - 4) * CT, CT), :],
                                        ps_router.rearrange("p (a h e) -> p a e h", a=CT, h=2), AX.X,
                                        ALU.add).then_inc(logits_ready, 1)

            def first_statistics(i):
                wait_apart(dve, x_loaded, i * 16 + 32)
                for j in range(CT):
                    a = acc[:, bass.ds((i + 1) * CT + j, 1), :].rearrange("p a t -> p (a t)")
                    nc.vector.bn_stats(st1[:, j], a).then_inc(st1_done, 1)
                for j in range(CT):
                    wait_apart(dve, st1_done, (i + 1) * CT + j + 1)
                    nc.vector.bn_aggr(mv1[:, j], st1[:, j]).then_inc(mv1_done, 1)
                dve.wait_ge(mv1_done, (i + 2) * CT)
                nc.vector.tensor_scalar(ve1[:], mv1[:, :, 1], LN_EPS, None, ALU.add).then_inc(ve1_ready, 1)

            def first_normalised(i, has):
                dve.wait_ge(rstd1_ready, i + 2)
                if has(0):
                    dve.wait_ge(gx_mm, i + 1)
                for j in range(CT):
                    a = acc[:, bass.ds((i + 1) * CT + j, 1), :].rearrange("p a t -> p (a t)")
                    nc.vector.tensor_scalar(in1[:, j], a, mv1[:, j, 0:1], rstd1[:, j:j + 1], ALU.subtract,
                                            ALU.mult).then_inc(in1_ready, 1)

            def turn(i, has):
                if at(i, 0):
                    dve.wait_ge(gates_loaded, 16 * GATES_LOADS)
                    dve.wait_ge(small_loaded, 16 * SMALL_LOADS)
                    router_weights_high()
                    first_statistics(0)
                if has(2):
                    dve.wait_ge(var_mm, i - 1)
                    nc.vector.tensor_scalar(veh[:], ps_var, LN_EPS, None, ALU.add).then_inc(veh_ready, 1)
                if has(3):
                    dve.wait_ge(rstd2_ready, i - 2)
                    nc.vector.scalar_tensor_tensor(nmr2[:], mv2[:, :, 0], -1.0, rstd2[:], ALU.mult, ALU.mult) \
                        .then_inc(nmr2_ready, 1)
                if at(i, NB + 2):
                    hidden(0, 0, 2)
                if has(2):
                    if has(3):
                        dve.wait_ge(hid_ready, i - 2)
                    nc.vector.scalar_tensor_tensor(z[:], tx[:], muh[:], gamma[:], ALU.subtract, ALU.mult) \
                        .then_inc(z1_done, 1)
                if has(1):
                    copy_probT(i, 1, has)
                if has(0):
                    row_maximum(i, 0)
                    row_maximum(i, 1)
                if has(1):
                    copy_probT(i, 3, has)
                if has(2):
                    dve.wait_ge(rstdh_ready, i - 1)
                    dve.wait_ge(z1_done, i - 1)
                    nc.vector.scalar_tensor_tensor(z[:], z[:], rstdh[:], beta[:], ALU.mult, ALU.add) \
                        .then_inc(z2_done, 1)
                if at(i, NB + 1):
                    hidden(0, 0, 1)
                if has(0):
                    row_maximum(i, 2)
                    row_maximum(i, 3)
                if has(4):
                    read_logits(i)
                if at(i, 3):
                    weights_scale(0, 0)
                if has(-1) and not at(i, 0):
                    first_statistics(i)
                if has(0):
                    dve.wait_ge(exp_done, i * TT + TT)
                    if at(i, 0):
                        first_normalised(i, has)
                    nc.vector.reciprocal(rinv[:], rsum[:]).then_inc(rinv_ready, 1)
                    dve.wait_ge(rinv_ready, i + 1)
                    for j in range(TT):
                        nc.vector.tensor_scalar(prob[:, j], prob[:, j], rinv[:, j:j + 1], None, ALU.mult) \
                            .then_inc(prob_ready, 1)
                if has(1):
                    wait_apart(dve, tx_ready, i)
                    nc.vector.bn_stats(sth[:], tx[:]).then_inc(sth_done, 1)
                    wait_apart(dve, sth_done, i)
                    nc.vector.bn_aggr(mvh[:], sth[:]).then_inc(mvh_ready, 1)
                if has(-1) and not at(i, 0):
                    first_normalised(i, has)
                if has(1):
                    dve.wait_ge(mu_mm, i)
                    nc.vector.tensor_copy(muh[:], ps_mu).then_inc(mu_read, 1)
                    dve.wait_ge(mu_read, i * 2 - 1)
                    nc.vector.tensor_tensor(dh[:], mvh[:, 0:1], muh[:], ALU.subtract).then_inc(mu_read, 1)
                    dve.wait_ge(mu_read, i * 2)
                    nc.vector.scalar_tensor_tensor(vh[:], dh[:], dh[:], mvh[:, 1:2], ALU.mult, ALU.add) \
                        .then_inc(vh_ready, 1)
                if has(3):
                    for m in range(2):
                        dve.wait_ge(xh_ready, (i - 3) * 2 + m + 1)
                        where = (slice(None), slice(2 * m, 2 * m + 2), bass.ds((i - 3) * C, C))
                        nc.vector.scalar_tensor_tensor(
                            xl[where], ps_tr[m][:].rearrange("p (k c) -> p k c", k=2), XSCALE, xh[where],
                            ALU.mult, ALU.subtract).then_inc(xl_ready, 1)
                if has(2):
                    dve.wait_ge(res_added, (i - 1) * CT)
                    for j in range(CT):
                        a = acc[:, bass.ds((i - 2) * CT + j, 1), :].rearrange("p a t -> p (a t)")
                        dve.wait_ge(out_mm, (i - 2) * CT + j + 1)
                        nc.vector.scalar_tensor_tensor(a, ps_out[j][:], gates[:, 0:1], a, ALU.mult, ALU.add) \
                            .then_inc(acc_added, 1)
                    for j in range(CT):
                        a = acc[:, bass.ds((i - 2) * CT + j, 1), :].rearrange("p a t -> p (a t)")
                        wait_apart(dve, acc_added, (i - 2) * CT + j + 1)
                        nc.vector.bn_stats(st2[:, j], a).then_inc(st2_done, 1)
                    for j in range(CT):
                        wait_apart(dve, st2_done, (i - 2) * CT + j + 1)
                        nc.vector.bn_aggr(mv2[:, j], st2[:, j]).then_inc(mv2_done, 1)
                    dve.wait_ge(mv2_done, (i - 1) * CT)
                    if has(3):
                        dve.wait_ge(xn2_ready, (i - 2) * CT)
                    nc.vector.tensor_scalar(ve2[:], mv2[:, :, 1], LN_EPS, None, ALU.add).then_inc(ve2_ready, 1)
                if at(i, 0):
                    router_weights_low()
                if at(i, 0):
                    weights_max(0, 0, (0,))
                if at(i, 1):
                    weights_max(0, 0, (1,))
                if at(i, 2):
                    weights_max(0, 0, (2,))

            dve.wait_ge(projT_mm, 1)
            nc.vector.tensor_copy(projT[:, 0:4, :].rearrange("p a l -> p (a l)"), ps_tr[0][:]).then_inc(projT_ready, 1)
            turns(dve, turn, after)
            read_logits(NB + 3)

            count = [0]

            def link(ins):
                count[0] += 1
                ins.then_inc(route_step, 1)
                dve.wait_ge(route_step, count[0])

            def per_token(n):
                return total[:, n, :].unsqueeze(2).broadcast_to([P, NT, E])

            Z, EXPZ, INH, DIST, W, FB, T1, T2, M1, M2 = range(10)
            pl = [plane[:, n] for n in range(10)]

            def route_distances():
                dve.wait_ge(logits_ready, NB)
                dve.wait_ge(const_ready, 3 + E)
                nc.vector.tensor_scalar(pl[Z], logits[:], unscale[:, ROUTER, 0:1], inv_temp[:], ALU.mult, ALU.mult) \
                    .then_inc(route_z, 1)
                dve.wait_ge(route_exp, 1)
                link(nc.vector.tensor_scalar(pl[EXPZ], pl[EXPZ], 1.0, None, ALU.add))
                link(nc.vector.reciprocal(pl[INH], pl[EXPZ]))
                link(nc.vector.tensor_scalar(pl[T2], pl[INH], GOLDEN_CENTER, None, ALU.subtract))
                nc.vector.scalar_tensor_tensor(pl[DIST], pl[T2], -1.0, pl[T2], ALU.mult, ALU.max) \
                    .then_inc(route_dist, 1)

            def route_zone():
                dve.wait_ge(route_z, 1)
                link(nc.vector.tensor_scalar(pl[T1], pl[Z], ZONE_LOW, None, ALU.is_ge))
                link(nc.vector.scalar_tensor_tensor(pl[T1], pl[Z], 0.0, pl[T1], ALU.is_le, ALU.mult))
                dve.wait_ge(route_exp, 3)
                link(nc.vector.tensor_tensor(pl[W], pl[W], pl[T1], ALU.mult))
                link(nc.vector.reduce_sum(total[:, 0, :], pl[W], AX.X))
                link(nc.vector.tensor_scalar(total[:, 0, :], total[:, 0, :], 1e-8, None, ALU.is_lt))
                link(nc.vector.tensor_copy(pl[T1], pl[FB]))

            def route_top(m):
                link(nc.vector.tensor_reduce(total[:, 1, :], pl[T1], AX.X, ALU.max))
                link(nc.vector.tensor_tensor(pl[T2], pl[T1], per_token(1), ALU.is_ge))
                link(nc.vector.tensor_tensor(pl[T2], pl[T2], rank[:], ALU.mult))
                link(nc.vector.tensor_reduce(total[:, 2, :], pl[T2], AX.X, ALU.max))
                link(nc.vector.tensor_tensor(pl[m], pl[T2], per_token(2), ALU.is_equal))
                link(nc.vector.scalar_tensor_tensor(pl[T1], pl[m], -2.0, pl[T1], ALU.mult, ALU.add))

            def route_fallback():
                link(nc.vector.tensor_tensor(pl[M1], pl[M1], pl[M2], ALU.add))
                link(nc.vector.tensor_tensor(pl[FB], pl[FB], pl[M1], ALU.mult))
                link(nc.vector.reduce_sum(total[:, 1, :], pl[FB], AX.X))
                link(nc.vector.tensor_scalar(total[:, 1, :], total[:, 1, :], 1e-8, None, ALU.max))
                link(nc.vector.reciprocal(total[:, 2, :], total[:, 1, :]))
                link(nc.vector.tensor_tensor(pl[FB], pl[FB], per_token(2), ALU.mult))
                link(nc.vector.tensor_tensor(pl[FB], pl[FB], per_token(0), ALU.mult))

            def route_mix():
                link(nc.vector.tensor_scalar(total[:, 3, :], total[:, 0, :], -1.0, 1.0, ALU.mult, ALU.add))
                link(nc.vector.tensor_tensor(pl[W], pl[W], per_token(3), ALU.mult))
                link(nc.vector.tensor_tensor(pl[W], pl[W], pl[FB], ALU.add))
                link(nc.vector.reduce_sum(total[:, 1, :], pl[W], AX.X))
                link(nc.vector.tensor_scalar(total[:, 1, :], total[:, 1, :], 1e-8, None, ALU.max))
                link(nc.vector.reciprocal(total[:, 2, :], total[:, 1, :]))
                link(nc.vector.tensor_scalar(total[:, 2, :], total[:, 2, :], gates[:, 1:2], None, ALU.mult))
                nc.vector.tensor_tensor(mix[:], pl[W], per_token(2), ALU.mult).then_inc(mix_ready, 1)
                dve.wait_ge(mix_ready, 1)

            def hidden_split(s, hp):
                dve.wait_ge(h_am_all, s + 1)
                power_scale(HIDDEN + hp, 1, h_scaling, s, XSCALE).then_inc(h_scaled, 1)
                dve.wait_ge(h_scaled, s + 1)
                dve.wait_ge(hh_ready, s + 1)
                nc.vector.scalar_tensor_tensor(
                    hl[hp][:].rearrange("p k n -> p (k n)"), hbuf[:].rearrange("p k n -> p (k n)"),
                    scale[:, HIDDEN + hp, 0:1], hh[hp][:].rearrange("p k n -> p (k n)"), ALU.mult, ALU.subtract) \
                    .then_inc(hl_ready, 1)

            def combine(s, e, u):
                hp, par, blk = u % 2, u // NBLK % 2, u % NBLK
                ei = slice(e, e + 1) if isinstance(e, int) else bass.ds(e, 1)
                nc.vector.tensor_scalar(coef[:, hp],
                                        mix[:, blk * TPB:(blk + 1) * TPB, ei].rearrange("p a e -> p (a e)"),
                                        unscale[:, HIDDEN + hp, 0:1], unscale[:, WEIGHTS + par, 2:3], ALU.mult,
                                        ALU.mult).then_inc(coef_ready, 1)
                dve.wait_ge(coef_ready, s + 1)
                for t in range(TPB):
                    dve.wait_ge(down_mm, s * TPB + t + 1)
                    a = acc[:, blk * TPB + t, :]
                    nc.vector.scalar_tensor_tensor(a, ps_down[t][:], coef[:, hp, t:t + 1], a, ALU.mult, ALU.add) \
                        .then_inc(combined, 1)

            def first():
                route_distances()
                hidden(0, 0, 3)
                route_zone()
                hidden_split(0, 0)
                hidden(1, 0, 0)
                route_top(M1)
                hidden(1, 0, 1)
                route_top(M2)
                hidden(1, 0, 2)
                route_fallback()
                hidden(1, 0, 3)
                hidden_split(1, 1)
                route_mix()
                combine(0, 0, 0)
                weights_max(1, 1)

            def step_turn(s, e, u, more):
                last = at(e, E - 1)
                local, other = u % NBLK, (u // NBLK + 1) % 2
                if more:
                    for f in range(KF):
                        hidden(s + 1, (u + 1) // NBLK % 2, f)
                if local == 1 and not last:
                    weights_scale(e + 1, other)
                if more:
                    hidden_split(s + 1, (u + 1) % 2)
                combine(s, e, u)
                if local == 0 and not last:
                    weights_max(e + 1, other)
                if local == 1 and not last:
                    weights_low(e + 1, other)

            steps(dve, first, step_turn, 1)

        @block.tensor
        def _(pe):
            pe.wait_ge(const_ready, 3)
            def transpose_weights(n):
                pe.wait_ge((proj_loaded, proj2_loaded)[n], 32)
                for a in range(4):
                    last = nc.tensor.transpose(ps_tr[n][:, a * P:(a + 1) * P], proj_raw[:, 4 * n + a, :], ident[:])
                last.then_inc(projT_mm, 1)

            transpose_weights(0)
            pe.wait_ge(projT_ready, 1)

            def turn(i, has):
                if has(0):
                    pe.wait_ge(in2_loaded, i * 16 + 16)
                    if has(1):
                        pe.wait_ge(exp_done, i * TT)
                    for k in range(CT):
                        last = nc.tensor.matmul(ps_theta[:], proj_w(0, k), in2[:, k], start=(k == 0), stop=(k == 1))
                    last.then_inc(theta_mm, 1)
                    pe.wait_ge(in1_ready, i * CT + CT)
                    for k in range(CT):
                        last = nc.tensor.matmul(ps_phi[:], proj_w(1, k), in1[:, k], start=(k == 0), stop=(k == 1))
                    last.then_inc(phi_mm, 1)
                if at(i, 0):
                    transpose_weights(1)
                if has(2):
                    pe.wait_ge(vh_ready, i - 1)
                    nc.tensor.matmul(ps_var, mean_w[:], vh[:], start=True, stop=True).then_inc(var_mm, 1)
                for half in range(2):
                    for j in (2 * half, 2 * half + 1):
                        if has(1):
                            if j == 0:
                                pe.wait_ge(prob_ready, i * TT)
                                if has(4):
                                    pe.wait_ge(xl_ready, (i - 3) * 2)
                            if j >= 2:
                                pe.wait_ge(probT_odd if j % 2 else probT_even, (i - 1) * 2 + j // 2)
                            for t in range(TT):
                                last = nc.tensor.transpose(ps_tr[j % 2][:, t * P:(t + 1) * P],
                                                           prob[:, t, j * P:(j + 1) * P], ident[:])
                            last.then_inc(probT_mm, 1)
                    for j in (2 * half, 2 * half + 1):
                        if has(0):
                            if j == 0:
                                pe.wait_ge(theta_ready, i + 1)
                                pe.wait_ge(phi_ready, i + 1)
                            if j < 2 and has(3):
                                pe.wait_ge(acc_added, (i - 2) * CT - j)
                            elif j == 0 and has(1):
                                pe.wait_ge(gx_ready, i)
                            nc.tensor.matmul(ps_score[j][:], thetaT[:, j * P:(j + 1) * P], phi[:], start=True,
                                             stop=True).then_inc(score_mm, 1)
                if has(4):
                    router(i)
                if has(1):
                    pe.wait_ge(gx_ready, i)
                    if has(2):
                        pe.wait_ge(tx_ready, i - 1)
                    for j in range(TT):
                        pe.wait_ge(probT_odd if j % 2 else probT_even, (i - 1) * 2 + j // 2 + 1)
                        last = nc.tensor.matmul(ps_tx[:], gx[:, j, :], probT[:, j], start=(j == 0), stop=(j == TT - 1))
                    last.then_inc(tx_mm, 1)
                if at(i, 0):
                    pe.wait_ge(projT_ready, 2)
                if has(0):
                    pe.wait_ge(exp_done, i * TT + 1)
                    for j in range(TT):
                        for k in range(CT):
                            last = nc.tensor.matmul(ps_gx[:, j * P:(j + 1) * P], in1[:, k, j * P:(j + 1) * P],
                                                    proj_w(2, k), start=(k == 0), stop=(k == 1))
                    last.then_inc(gx_mm, 1)
                if has(3):
                    pe.wait_ge(xn2_ready, (i - 2) * CT)
                    for m in range(2):
                        if has(1):
                            pe.wait_ge(probT_odd if m else probT_even, i * 2)
                        for k in range(2):
                            for j in range(CT):
                                col = k * C + j * P
                                last = nc.tensor.transpose(ps_tr[m][:, col:col + P],
                                                           xn2[:, j, (2 * m + k) * P:(2 * m + k + 1) * P], ident[:])
                        last.then_inc(xT_mm, 1)
                if has(1):
                    pe.wait_ge(mvh_ready, i)
                    if has(2):
                        pe.wait_ge(veh_ready, i - 1)
                    if has(4):
                        pe.wait_ge(logits_ready, i - 3)
                    nc.tensor.matmul(ps_mu, mean_w[:], mvh[:, 0:1], start=True, stop=True).then_inc(mu_mm, 1)
                if has(2):
                    pe.wait_ge(hid_ready, i - 1)
                    for j in range(CT):
                        if has(0) and j == 0:
                            pe.wait_ge(exp_done, i * TT + 2)
                        if has(0) and j == 1:
                            pe.wait_ge(gx_ready, i + 1)
                        if has(3):
                            pe.wait_ge(acc_added, (i - 3) * CT + j + 1)
                        if at(i, NB + 1):
                            pe.wait_ge(h_done, 2)
                        nc.tensor.matmul(ps_out[j][:], out_wT(j), hid[:], start=True, stop=True).then_inc(out_mm, 1)
            def router(i):
                pe.wait_ge(xl_ready, (i - 3) * 2)
                pe.wait_ge(wrh_ready, 1)
                pe.wait_ge(wrl_ready, 1)
                if not isinstance(i, int) or i < NB + 2:
                    pe.wait_ge(veh_ready, i - 1)
                else:
                    pe.wait_ge(logits_ready, i - 4)
                for j in range(CT):
                    tok = bass.ds(((i - 4) * CT + j) * P, P)
                    o = ps_router[:, j * 2 * E:(j + 1) * 2 * E]
                    for k in range(KD):
                        w = wr2[:, k].rearrange("p h e -> p (h e)")
                        nc.tensor.matmul(o, xh[:, k, tok], w, start=(k == 0), stop=False)
                        last = nc.tensor.matmul(o, xl[:, k, tok], w, start=False, stop=(k == KD - 1))
                last.then_inc(router_mm, 1)

            def out_wT(j):
                return projT[:, 6 + j, :]

            def gate_up(s, e, blk, par, tiles=range(KF), which=range(2)):
                tok = slice(blk * TB, (blk + 1) * TB)
                for f in tiles:
                    cols = slice(f * P, (f + 1) * P)
                    for w in which:
                        ps, done, used = ((ps_gate, gate_mm, silu_ready), (ps_up, up_mm, h_done))[w]
                        if blk == 0 and f == 0:
                            pe.wait_ge(wh_ready, e * 3 + w + 1)
                            pe.wait_ge(wl_ready, e * 3 + w + 1)
                        if not isinstance(s, int) or s * KF + f >= 2:
                            pe.wait_ge(used, s * KF + f - 1)
                        for k in range(KD):
                            a, b = wh[par][:, w, k, cols], wl[par][:, w, k, cols]
                            nc.tensor.matmul(ps[f % 2][:], a, xh[:, k, tok], start=(k == 0), stop=False)
                            nc.tensor.matmul(ps[f % 2][:], a, xl[:, k, tok], start=False, stop=False)
                            last = nc.tensor.matmul(ps[f % 2][:], b, xh[:, k, tok], start=False, stop=(k == KD - 1))
                        last.then_inc(done, 1)

            def down(s, e, u):
                hp, par = u % 2, u // NBLK % 2
                if at(s, STEPS - 1):
                    pe.wait_ge(combined, s * TPB)
                if u % NBLK == 0:
                    pe.wait_ge(wh_ready, e * 3 + 3)
                    pe.wait_ge(wl_ready, e * 3 + 3)
                pe.wait_ge(hh_ready, s + 1)
                pe.wait_ge(hl_ready, s + 1)
                for t in range(TPB):
                    rows = slice(t * P, (t + 1) * P)
                    for k in range(KF):
                        a, b = hh[hp][:, k, rows], hl[hp][:, k, rows]
                        nc.tensor.matmul(ps_down[t][:], a, wh[par][:, 2, k, :], start=(k == 0), stop=False)
                        nc.tensor.matmul(ps_down[t][:], a, wl[par][:, 2, k, :], start=False, stop=False)
                        last = nc.tensor.matmul(ps_down[t][:], b, wh[par][:, 2, k, :], start=False,
                                                stop=(k == KF - 1))
                    last.then_inc(down_mm, 1)

            def step_turn(s, e, u, more):
                if more:
                    n = u + 1
                    gate_up(s + 1, e + (1 if n % NBLK == 0 else 0), n % NBLK, n // NBLK % 2)
                down(s, e, u)

            def after(i):
                if at(i, NB - 1):
                    pe.wait_ge(exp_done, NB * TT)
                    gate_up(0, 0, 0, 0, range(0, 1))
                if at(i, NB):
                    pe.wait_ge(acc_added, (NB - 1) * CT)
                    gate_up(0, 0, 0, 0, range(1, 2))
                if at(i, NB + 1):
                    gate_up(0, 0, 0, 0, range(2, 3))
                if at(i, NB + 2):
                    pe.wait_ge(acc_added, NB * CT)
                    gate_up(0, 0, 0, 0, range(3, 4), (0,))

            turns(pe, turn, after)
            router(NB + 3)
            steps(pe, lambda: gate_up(0, 0, 0, 0, range(3, 4), (1,)), step_turn)


_INS = ['x', 'ctx_2048', 'g_xattn', 'g_ffn', 'L0_xattn_theta_w', 'L0_xattn_theta_b', 'L0_xattn_phi_w',
        'L0_xattn_phi_b', 'L0_xattn_g_w', 'L0_xattn_g_b', 'L0_xattn_ln_gamma', 'L0_xattn_ln_beta',
        'L0_xattn_out_w', 'L0_xattn_out_b', 'L0_ffn_Wg', 'L0_ffn_Wu', 'L0_ffn_Wd', 'L0_ffn_Wr',
        'L0_ffn_temperature']


def kernel(**inputs):
    import numpy as _np
    import concourse.bacc as _bacc
    from concourse.bass_utils import run_bass_kernel_spmd as _run

    nc = _bacc.Bacc("TRN2", target_bir_lowering=False, num_devices=1)
    arrays, args = {}, []
    for name in _INS:
        a = _np.ascontiguousarray(inputs[name])
        arrays[f"in_{name}_dram"] = a
        args.append(nc.dram_tensor(f"in_{name}_dram", a.shape, mybir.dt.from_np(a.dtype), kind="ExternalInput").ap())
    args.append(nc.dram_tensor("out_0_dram", inputs['x'].shape, F32, kind="ExternalOutput").ap())
    build(nc, *args)
    r = _run(nc, [arrays], core_ids=[0])
    return r.results[0]["out_0_dram"]
```
